# Optimizing a Trainium2 kernel written in Bass

```python
import numpy as np
import jax
import jax.numpy as jnp

def _softmax(x, axis=-1):
    return jax.nn.softmax(x, axis=axis)

def _gelu(x):
    return jax.nn.gelu(x, approximate=True)

def _silu(x):
    return jax.nn.silu(x)

def _sigmoid(x):
    return jax.nn.sigmoid(x)

def _layernorm(x, axis=-1, eps=1e-05):
    m = jnp.mean(x, axis=axis, keepdims=True)
    v = jnp.var(x, axis=axis, keepdims=True)
    return (x - m) / jnp.sqrt(v + eps)

def _scatter_add(tgt, idx, src, axis=0):
    return tgt.at[idx].add(src)

def _segment_sum(src, seg, n):
    return jax.ops.segment_sum(src, seg, n)
kernel_name = 'mk_sandwich_d1_jaxref_r8_4f4f7a'

def setup_inputs(seed: int=0):
    np.random.seed(seed)
    _w = jnp.asarray

    def _L0_attn_setup():
        import jax, jax.numpy as jnp
        import numpy as np
        B, S, D = (4, 128, 128)
        H, M = (16, 64)
        HD = D // H
        key = jax.random.key(seed)
        ks = jax.random.split(key, 8)
        return {'query': jax.random.normal(ks[0], (B, S, D), dtype=jnp.float32), 'w_qkv': jax.random.normal(ks[1], (3 * D, D), dtype=jnp.float32) * D ** (-0.5), 'b_qkv': jax.random.normal(ks[2], (3 * D,), dtype=jnp.float32) * 0.02, 'w_out': jax.random.normal(ks[3], (D, D), dtype=jnp.float32) * D ** (-0.5), 'b_out': jax.random.normal(ks[4], (D,), dtype=jnp.float32) * 0.02, 'freq_q': jax.random.normal(ks[5], (H, M, HD), dtype=jnp.float32), 'freq_k': jax.random.normal(ks[6], (H, M, HD), dtype=jnp.float32), 'freq_v': jax.random.normal(ks[7], (H, M, HD), dtype=jnp.float32)}
    _L0_attn_in = _L0_attn_setup()

    def _L0_ffn_setup():
        import jax, jax.numpy as jnp
        import numpy as np
        B, S, H, F, E, K = (2, 128, 128, 256, 8, 2)
        key = jax.random.key(seed)
        ks = jax.random.split(key, 5)
        scale_h = 1.0 / np.sqrt(H)
        scale_f = 1.0 / np.sqrt(F)
        return {'inputs': jax.random.normal(ks[0], (B, S, H), dtype=jnp.float32), 'router_w': jax.random.normal(ks[1], (H, E), dtype=jnp.float32) * scale_h, 'w1': jax.random.normal(ks[2], (E, H, F), dtype=jnp.float32) * scale_h, 'w3': jax.random.normal(ks[3], (E, H, F), dtype=jnp.float32) * scale_h, 'w2': jax.random.normal(ks[4], (E, F, H), dtype=jnp.float32) * scale_f}
    _L0_ffn_in = _L0_ffn_setup()
    _d = {'L0_attn_query': _L0_attn_in['query'], 'L0_attn_w_qkv': _L0_attn_in['w_qkv'], 'L0_attn_b_qkv': _L0_attn_in['b_qkv'], 'L0_attn_w_out': _L0_attn_in['w_out'], 'L0_attn_b_out': _L0_attn_in['b_out'], 'L0_attn_freq_q': _L0_attn_in['freq_q'], 'L0_attn_freq_k': _L0_attn_in['freq_k'], 'L0_attn_freq_v': _L0_attn_in['freq_v'], 'L0_ffn_router_w': _L0_ffn_in['router_w'], 'L0_ffn_w1': _L0_ffn_in['w1'], 'L0_ffn_w3': _L0_ffn_in['w3'], 'L0_ffn_w2': _L0_ffn_in['w2']}
    _x0 = _d['L0_attn_query']
    _d['L0_attn_query'] = jax.random.normal(jax.random.fold_in(jax.random.key(seed), 1), (8, 512, 128), dtype=_x0.dtype)
    del _x0
    return _d

def reference(L0_attn_query, L0_attn_w_qkv, L0_attn_b_qkv, L0_attn_w_out, L0_attn_b_out, L0_attn_freq_q, L0_attn_freq_k, L0_attn_freq_v, L0_ffn_router_w, L0_ffn_w1, L0_ffn_w3, L0_ffn_w2):

    def _L0_attn_ref(query, w_qkv, b_qkv, w_out, b_out, freq_q, freq_k, freq_v):
        import jax, jax.numpy as jnp
        import numpy as np
        B, S, D = (4, 128, 128)
        H, M = (16, 64)
        HD = D // H
        b, s, d = query.shape
        h, m, hd = freq_q.shape
        fft_base = jnp.fft.fft(jnp.eye(s, dtype=jnp.float32)).astype(jnp.complex64)
        qkv = query @ w_qkv.T + b_qkv
        q, k, v = jnp.split(qkv, 3, axis=-1)

        def heads(x):
            return x.reshape(b, s, h, hd).transpose(0, 2, 1, 3)
        q, k, v = (heads(q), heads(k), heads(v))

        def to_freq(x):
            xc = x.astype(jnp.complex64)
            return jnp.einsum('bhsd,fs->bhfd', xc, jnp.conj(fft_base))

        def filt(xf, w):
            xt = xf[:, :, :m] * w.astype(jnp.complex64)[None]
            return jnp.pad(xt, ((0, 0), (0, 0), (0, s - m), (0, 0)))
        q_fft = filt(to_freq(q), freq_q)
        k_fft = filt(to_freq(k), freq_k)
        v_fft = filt(to_freq(v), freq_v)
        scores = jnp.sum(jnp.real(q_fft * jnp.conj(k_fft)), axis=-1, keepdims=True)
        attn = jax.nn.softmax(scores, axis=2)
        out_fft = attn.astype(jnp.complex64) * v_fft
        out = jnp.real(jnp.einsum('bhfd,fs->bhsd', out_fft, fft_base))
        out = out.transpose(0, 2, 1, 3).reshape(b, s, d)
        return out @ w_out.T + b_out

    def _L0_ffn_ref(inputs, router_w, w1, w3, w2):
        import jax, jax.numpy as jnp
        import numpy as np
        B, S, H, F, E, K = (2, 128, 128, 256, 8, 2)
        b, s, h = inputs.shape
        x = inputs.reshape(-1, h)
        logits = x @ router_w
        top_vals, top_idx = jax.lax.top_k(logits, K)
        importance = jax.nn.softmax(top_vals.astype(jnp.float32), axis=-1).astype(x.dtype)
        one_hot = top_idx[..., None] == jnp.arange(E)[None, None, :]
        combine = jnp.sum(jnp.where(one_hot, importance[..., None], 0.0), axis=1)
        gate = jax.nn.silu(jnp.einsum('th,ehf->etf', x, w1))
        up = jnp.einsum('th,ehf->etf', x, w3)
        expert_out = jnp.einsum('etf,efh->eth', gate * up, w2)
        out = jnp.einsum('te,eth->th', combine, expert_out)
        return out.reshape(b, s, h)
    x = L0_attn_query
    x = x + _layernorm(_L0_attn_ref(_layernorm(x, axis=-1), L0_attn_w_qkv, L0_attn_b_qkv, L0_attn_w_out, L0_attn_b_out, L0_attn_freq_q, L0_attn_freq_k, L0_attn_freq_v), axis=-1)
    x = x + _layernorm(_L0_ffn_ref(_layernorm(x, axis=-1), L0_ffn_router_w, L0_ffn_w1, L0_ffn_w3, L0_ffn_w2), axis=-1)
    return x

_drawn_inputs = setup_inputs


def setup_inputs(seed=0):
    import zlib

    import numpy as np

    out = dict(_drawn_inputs(seed))
    spreads = {}
    factors = {'L0_attn_b_out': 3.857}
    for name, (base, spread) in spreads.items():
        noise = np.random.default_rng([zlib.crc32(name.encode()), seed]).standard_normal(out[name].shape)
        drawn = base * np.exp(spread * noise) if base else spread * noise
        out[name] = jnp.asarray(drawn.astype(out[name].dtype))
    for name, factor in factors.items():
        out[name] = (out[name] * factor).astype(out[name].dtype)
    return out
```

```python
from contextlib import ExitStack

import numpy as np

import concourse.bass as bass
from concourse import mybir

ALU = mybir.AluOpType
ACT = mybir.ActivationFunctionType
AX = mybir.AxisListType
F32 = mybir.dt.float32
F32R = mybir.dt.float32r
BF16 = mybir.dt.bfloat16
I32 = mybir.dt.int32

P = 128
B, S, D = 8, 512, 128
H, M, HD = 16, 64, 8
E, F = 8, 256
FC = F // P
EPS = 1e-5
CUT = float(S - M)

TS = S // P
SEQS = 2
NG = B // SEQS
TG = TS * SEQS
NT = NG * TG
STEP = 6
ET = 24
TURNS = NG * ET // STEP
TPG = ET // STEP
ROW = 8
AHEAD = 3
SLOTS = ET * P
HALF = STEP // 2
ZLAG = TPG + 1
NLAG = ZLAG + TPG
ZT = TG // TPG
BIG = 3.0e38

assert SEQS * TS * P * 2 // P + E - 1 <= ET and ET % STEP == 0 and STEP % 2 == 0


def at_least(eng, sem, n):
    if isinstance(n, int) and n <= 0:
        return
    eng.wait_ge(sem, n)


def build(nc, x_in, wqkv_in, bqkv_in, wout_in, bout_in, fq_in, fk_in, fv_in, rw_in, w13_in, w2_in,
          ftab_in, ginv_in, ident_in, tri_in, rows_in, out):
    with ExitStack() as ctx:
        ctx.enter_context(nc.allow_low_precision(reason="sums of small whole numbers, kept as integers"))

        def sb(name, shape, dt=F32):
            return ctx.enter_context(nc.sbuf_tensor(name, shape, dt))

        def bank(name):
            return ctx.enter_context(nc.psum_tensor(name, [P, 512], F32))

        def sem(name):
            return ctx.enter_context(nc.semaphore(name))

        ftab = sb("ftab", [P, TS, P])
        ginv = sb("ginv", [P, S])
        ident = sb("ident", [P, P])
        tri_f = sb("tri_f", [P, P])
        tri = sb("tri", [P, P], BF16)
        ones = sb("ones", [P, P], BF16)
        fold = sb("fold", [P, M])
        rows = sb("rows", [P, 8 + 64 + TPG * ROW * 7])
        e_down = rows[:, 0:8]
        t_keep = rows[:, 8:72]
        j_row = rows[:, 72:72 + TPG * ROW * 7]
        eps = sb("eps", [P, 1])
        wqkv = sb("wqkv", [P, 3 * D])
        bqkv = sb("bqkv", [P, 3 * D])
        wout = sb("wout", [P, D])
        bout = sb("bout", [P, D])
        fq = sb("fq", [P, D])
        fk = sb("fk", [P, D])
        fv = sb("fv", [P, D])
        fqk = sb("fqk", [P, D])
        rw = sb("rw", [P, E])
        w13 = sb("w13", [P, E * 2 * F])
        w13h = sb("w13h", [P, E * 2 * F], F32R)
        w13l = sb("w13l", [P, E * 2 * F], F32R)
        w2 = sb("w2", [P, E * 2 * F])
        zero = sb("zero", [P, ET * P])

        x = sb("x", [P, NT, D])
        shift2 = sb("shift2", [P, NT])

        st1 = sb("st1", [P, TG, 6])
        mean1 = sb("mean1", [P, TG])
        dif1 = sb("dif1", [P, TG])
        m2_1 = sb("m2_1", [P, TG])
        sq1 = sb("sq1", [P, TG])
        var1 = sb("var1", [P, TG])
        sd1 = sb("sd1", [P, TG])
        r1 = sb("r1", [P, TG])
        nm1 = sb("nm1", [P, TG])
        xn = sb("xn", [P, TG, D])
        xft = sb("xft", [P, SEQS, P])
        qkv = sb("qkv", [P, SEQS, 3 * D])
        prod = sb("prod", [P, SEQS, D])
        prodw = sb("prodw", [P, SEQS, D])
        vw = sb("vw", [P, SEQS, D])
        red = sb("red", [P, SEQS * H])
        NH = SEQS * H
        mx = sb("mx", [NH, 1])
        nmx = sb("nmx", [NH, 1])
        ex = sb("ex", [NH, M])
        exs = sb("exs", [NH, 1])
        ex0 = sb("ex0", [NH, 1])
        tot = sb("tot", [NH, 1])
        rtot = sb("rtot", [NH, 1])
        attn = sb("attn", [NH, 2, M])
        of = sb("of", [P, SEQS, D])
        oft = sb("oft", [P, SEQS, P])
        zs = sb("zs", [P, SEQS, D])

        st2 = sb("st2", [P, TG, 6])
        mean2 = sb("mean2", [P, TG])
        dif2 = sb("dif2", [P, TG])
        m2_2 = sb("m2_2", [P, TG])
        sq2 = sb("sq2", [P, TG])
        var2 = sb("var2", [P, TG])
        sd2 = sb("sd2", [P, TG])
        r2 = sb("r2", [P, TG])
        st3 = sb("st3", [P, TG, 6])
        mean3 = sb("mean3", [P, TG])
        dif3 = sb("dif3", [P, TG])
        m2_3 = sb("m2_3", [P, TG])
        sq3 = sb("sq3", [P, TG])
        var3 = sb("var3", [P, TG])
        sd3 = sb("sd3", [P, TG])
        r3 = sb("r3", [P, TG])
        nm3 = sb("nm3", [P, TG])
        xn2 = sb("xn2", [P, TG, D])
        xn2s = sb("xn2s", [P, TG, D])
        xn2t = sb("xn2t", [P, SEQS, S])

        m1 = sb("m1", [P, TG])
        m2 = sb("m2", [P, TG])
        i1 = sb("i1", [P, TG])
        i2 = sb("i2", [P, TG])
        eq = sb("eq", [P, TG, E])
        eqd = sb("eqd", [P, TG, E])
        oh1 = sb("oh1", [P, TG, E])
        oh2 = sb("oh2", [P, TG, E])
        rest = sb("rest", [P, TG, E])
        gap = sb("gap", [P, NT])
        e2 = sb("e2", [P, NT])
        e2p = sb("e2p", [P, NT])
        wt1 = sb("wt1", [P, NT])
        wt2 = sb("wt2", [P, NT])
        cnt = sb("cnt", [P, E, TG], BF16)
        inc = sb("inc", [P, E, TG])
        pos = sb("pos", [P, E, TG])
        pos2 = sb("pos2", [P, E, TG])
        up = sb("up", [P, E], I32)
        tiles = sb("tiles", [P, E], I32)
        cum = sb("cum", [P, E])
        base = sb("base", [P, E])
        slot = sb("slot", [P, E, TG])
        pick1 = sb("pick1", [P, TG, E])
        pick2 = sb("pick2", [P, TG, E])
        slots = sb("slots", [P, NG, 2, TG], I32)
        before = sb("before", [1, TPG * ROW * 7])
        expert = sb("expert", [1, TPG * ROW])
        columns = sb("columns", [1, TURNS * ROW], I32)

        xe = sb("xe", [P, STEP, D])
        xh = sb("xh", [P, 2, P], F32R)
        xl = sb("xl", [P, 2, P], F32R)
        gate = sb("gate", [P, 2, F])
        hid = sb("hid", [P, 2, F])
        hidt = sb("hidt", [P, 2, F])
        ye = sb("ye", [P, STEP, D])

        ya = sb("ya", [P, 2 * TG, D])
        yb = sb("yb", [P, 2 * TG, D])
        za = sb("za", [P, 2 * TG, D])
        stz = sb("stz", [P, NT, 6])
        meanz = sb("meanz", [P, NT])
        difz = sb("difz", [P, NT])
        m2_z = sb("m2_z", [P, NT])
        sqz = sb("sqz", [P, NT])
        varz = sb("varz", [P, NT])
        var = sb("var", [P, NT])
        rz = sb("rz", [P, NT])
        cz = sb("cz", [P, NT])
        shift = sb("shift", [P, NT])
        half = sb("half", [P, TG])
        zn = sb("zn", [P, NT, D])

        pb = [bank(f"pb{i}") for i in range(8)]

        xg = [nc.dram_tensor(f"xg{g}", [SLOTS, D], F32, kind="Internal").ap() for g in range(NG)]
        yg = [nc.dram_tensor(f"yg{g}", [SLOTS, D], F32, kind="Internal").ap() for g in range(NG)]

        s_held = sem("waits_passed")
        s_x = sem("x_loaded")
        s_wa = sem("attention_weights_loaded")
        s_we = sem("expert_weights_loaded")
        s_const = sem("constants_ready")
        s_halves = sem("exponents_ready")
        s_fqk = sem("filters_multiplied")
        s_w13 = sem("w13_split")
        s_zero = sem("zero_tile_ready")
        s_xgz = sem("slots_zeroed")
        s_st1 = sem("stats1")
        s_half1 = sem("halves_joined1")
        s_sq1 = sem("difference_squared1")
        s_var1 = sem("variance1")
        s_sd1 = sem("deviation1")
        s_r1 = sem("reciprocal1")
        s_nm1 = sem("shift1_ready")
        s_xn = sem("xn_ready")
        s_dft = sem("dft_done")
        s_xft = sem("xft_copied")
        s_qkvp = sem("qkv_done")
        s_qkv = sem("qkv_biased")
        s_prod = sem("qk_product")
        s_prodw = sem("qk_filtered")
        s_vw = sem("v_filtered")
        s_red = sem("qk_summed")
        s_sc = sem("scores_done")
        s_mx = sem("max_taken")
        s_nmx = sem("max_negated")
        s_ex = sem("exp_done")
        s_tot = sem("sum_done")
        s_rtot = sem("sum_inverted")
        s_attn = sem("attention_ready")
        s_at = sem("attention_turned")
        s_of = sem("of_ready")
        s_oftp = sem("of_turned")
        s_oft = sem("oft_copied")
        s_zp = sem("z_done")
        s_zs = sem("z_biased")
        s_y = sem("y_done")
        s_st2 = sem("stats2")
        s_half2 = sem("halves_joined2")
        s_sq2 = sem("difference_squared2")
        s_var2 = sem("variance2")
        s_sd2 = sem("deviation2")
        s_r2 = sem("reciprocal2")
        s_x1 = sem("x1_ready")
        s_st3 = sem("stats3")
        s_half3 = sem("halves_joined3")
        s_sq3 = sem("difference_squared3")
        s_var3 = sem("variance3")
        s_sd3 = sem("deviation3")
        s_r3 = sem("reciprocal3")
        s_nm3 = sem("shift3_ready")
        s_xn2 = sem("xn2_ready")
        s_rows = sem("rows_copied")
        s_xn2p = sem("xn2_turned")
        s_xn2t = sem("xn2t_copied")
        s_lg = sem("logits_done")
        s_top = sem("top2_steps")
        s_cnt = sem("counts_ready")
        s_pfx = sem("prefix_done")
        s_rt = sem("route_steps")
        s_slots = sem("slots_ready")
        s_cols = sem("columns_ready")
        s_scat = sem("rows_scattered")
        s_gap = sem("gaps_ready")
        s_e2 = sem("gap_exp")
        s_wt = sem("weights_of_pairs")
        s_xeA = sem("rows_loaded_a")
        s_xeB = sem("rows_loaded_b")
        s_xt = sem("tile_turned")
        s_xh = sem("tile_high")
        s_xl = sem("tile_low")
        s_gu = sem("gate_up_done")
        s_silu = sem("silu_done")
        s_h = sem("hidden_ready")
        s_ht = sem("hidden_turned")
        s_hc = sem("hidden_copied")
        s_dn = sem("down_done")
        s_ye = sem("tile_out")
        s_stA = sem("tiles_stored_a")
        s_stB = sem("tiles_stored_b")
        s_gat = [sem("pair_gathered_even"), sem("pair_gathered_odd")]
        s_za = sem("first_weighted")
        s_z = sem("sum_ready")
        s_stz = sem("stats_z")
        s_halfz = sem("halves_joined_z")
        s_sqz = sem("difference_squared_z")
        s_sumz = sem("variance_summed_z")
        s_var = sem("variance_z")
        s_rz = sem("rsqrt_z")
        s_cz = sem("shift_z")
        s_zn = sem("z_scaled")
        s_out = sem("out_ready")
        s_stored = sem("out_stored")

        x_dram = x_in.rearrange("(g t p) d -> g p t d", p=P, t=TG)
        out_dram = out.rearrange("(k t p) d -> k p t d", p=P, t=TG // 2)
        N_ATT, N_EXP = 13, 2
        TOP, RT = 11, 11

        block = ctx.enter_context(nc.Block())

        @block.sync
        def _(sp):
            for g in range(NG):
                at_least(sp, s_x, 16 * g)
                sp.dma_start(x[:, g * TG:(g + 1) * TG, :], x_dram[g]).then_inc(s_x, 16)
                if g == 0:
                    sp.dma_start(w13[:], w13_in).then_inc(s_we, 16)
                    sp.dma_start(w2[:].rearrange("p (e n) -> p e n", n=2 * F)[:, :, 0:FC * D],
                                 w2_in.rearrange("p (e n) -> p e n", n=FC * D)).then_inc(s_we, 16)
            sp.wait_ge(s_zero, 1)
            for g in range(NG):
                sp.dma_start(xg[g].rearrange("(p j) d -> p (j d)", p=P), zero[:]).then_inc(s_xgz, 16)

            def tiles_of(dram, turn, half):
                g, r = turn // TPG, (turn % TPG * STEP + half * HALF) * P
                return dram[g][r:r + HALF * P, :].rearrange("(j p) d -> p j d", p=P)

            def load(turn, half):
                if turn % TPG == 0:
                    sp.wait_ge(s_scat, 16 * 2 * TG * (turn // TPG + 1))
                at_least(sp, s_xt, STEP * (turn - 1) + HALF * (half + 1))
                sp.dma_start(xe[:, half * HALF:(half + 1) * HALF, :], tiles_of(xg, turn, half)).then_inc(
                    (s_xeA, s_xeB)[half], 16)

            def store(turn, half):
                sp.wait_ge(s_ye, STEP * turn + HALF * (half + 1))
                sp.dma_start(tiles_of(yg, turn, half), ye[:, half * HALF:(half + 1) * HALF, :]).then_inc(
                    (s_stA, s_stB)[half], 16)

            def store_out(k):
                sp.wait_ge(s_out, (k + 1) * TG // 2)
                sp.dma_start(out_dram[k], x[:, k * TG // 2:(k + 1) * TG // 2, :]).then_inc(s_stored, 16)

            stored = 0
            load(0, 0)
            load(0, 1)
            for turn in range(TURNS):
                if turn:
                    store(turn - 1, 1)
                if turn < TURNS - 1:
                    load(turn + 1, 0)
                store(turn, 0)
                if turn < TURNS - 1:
                    load(turn + 1, 1)
                if turn >= NLAG + 2 and turn % 2 == 1:
                    store_out(stored)
                    stored += 1
            store(TURNS - 1, 1)
            while stored < 2 * NG:
                store_out(stored)
                stored += 1
            sp.wait_ge(s_stored, 16 * 2 * NG)

        @block.gpsimd
        def _(pool):
            nc.gpsimd.memset(zero[:], 0.0).then_inc(s_zero, 1)
            nc.gpsimd.memset(half[:], -0.5).then_inc(s_halves, 1)
            pool.wait_ge(s_xgz, 16 * NG)
            for g in range(NG):
                pool.wait_ge(s_xn2, TG * (g + 1))
                at_least(pool, s_scat, 16 * 2 * TG * g)
                nc.gpsimd.tensor_copy(xn2s[:], xn2[:]).then_inc(s_rows, 1)
                pool.wait_ge(s_slots, 2 * (g + 1))
                pool.wait_ge(s_rows, g + 2)
                for t in range(TG):
                    for k in range(2):
                        pool.indirect_dma_start(
                            out=xg[g], out_offset=bass.IndirectOffsetOnAxis(ap=slots[:, g, k, t:t + 1], axis=0),
                            in_=xn2s[:, t, :], in_offset=None).then_inc(s_scat, 16)
            for g in range(NG):
                pool.wait_ge(s_stA, 16 * TPG * (g + 1))
                pool.wait_ge(s_stB, 16 * TPG * (g + 1))
                for t in range(TG):
                    k = g * TG + t
                    at_least(pool, s_out, TG * (g - 1) if t == 0 else 0)
                    at_least(pool, s_gat[t % 2], 32 * (k // 2))
                    for i, y in enumerate((ya, yb)):
                        pool.indirect_dma_start(
                            out=y[:, k % (2 * TG), :], out_offset=None, in_=yg[g],
                            in_offset=bass.IndirectOffsetOnAxis(ap=slots[:, g, i, t:t + 1], axis=0),
                        ).then_inc(s_gat[t % 2], 16)
                pool.wait_ge(s_halves, 1)
                pool.wait_ge(s_var, g + 1)
                nc.gpsimd.tensor_tensor(rz[:, g * TG:(g + 1) * TG], var[:, g * TG:(g + 1) * TG], half[:],
                                        ALU.pow).then_inc(s_rz, 1)

        @block.scalar
        def _(act):
            for dst, src in ((ftab[:], ftab_in.rearrange("(t p) f -> p t f", p=P)), (wqkv[:], wqkv_in),
                             (bqkv[:], bqkv_in), (fq[:], fq_in), (fk[:], fk_in), (fv[:], fv_in),
                             (ident[:], ident_in), (ginv[:], ginv_in), (wout[:], wout_in), (bout[:], bout_in),
                             (rw[:], rw_in), (tri_f[:], tri_in), (rows[:], rows_in)):
                act.dma_start(dst, src).then_inc(s_wa, 16)
            act.wait_ge(s_const, 1)
            act.sem_inc(s_rows, 1)

            def step(f, b):
                if b is not None:
                    act.wait_ge(s_oftp, b + 1)
                    nc.scalar.activation(oft[:], pb[4][:, 0:SEQS * P], ACT.Copy).then_inc(s_oft, 1)
                if f is not None:
                    act.wait_ge(s_var1, f + 1)
                    nc.scalar.activation(sd1[:], var1[:], ACT.Sqrt, bias=eps[:], scale=1.0 / D).then_inc(s_sd1, 1)
                    act.wait_ge(s_nm1, f + 1)
                    for t in range(TG):
                        nc.scalar.activation(xn[:, t, :], x[:, bass.ds(f * TG + t, 1), :].rearrange("p a d -> p (a d)"),
                                             ACT.Identity, bias=nm1[:, t:t + 1], scale=r1[:, t:t + 1]).then_inc(s_xn, 1)
                if b is not None:
                    act.wait_ge(s_var2, b + 1)
                    nc.scalar.activation(sd2[:], var2[:], ACT.Sqrt, bias=eps[:], scale=1.0 / D).then_inc(s_sd2, 1)
                if f is not None:
                    act.wait_ge(s_dft, f + 1)
                    nc.scalar.activation(xft[:], pb[0][:, 0:SEQS * P], ACT.Copy).then_inc(s_xft, 1)
                if b is not None:
                    act.wait_ge(s_var3, b + 1)
                    nc.scalar.activation(sd3[:], var3[:], ACT.Sqrt, bias=eps[:], scale=1.0 / D).then_inc(s_sd3, 1)
                    act.wait_ge(s_nm3, b + 1)
                    act.wait_ge(s_rows, b + 1)
                    for t in range(TG):
                        nc.scalar.activation(xn2[:, t, :], x[:, bass.ds(b * TG + t, 1), :].rearrange("p a d -> p (a d)"),
                                             ACT.Identity, bias=nm3[:, t:t + 1], scale=r3[:, t:t + 1]).then_inc(s_xn2, 1)
                    for q in range(SEQS):
                        act.wait_ge(s_xn2p, SEQS * b + q + 1)
                        nc.scalar.activation(xn2t[:, q, :], pb[5 + q][:], ACT.Copy).then_inc(s_xn2t, 1)
                if f is not None:
                    act.wait_ge(s_nmx, f + 1)
                    nc.scalar.activation(ex[:], pb[3][0:NH, 0:M], ACT.Exp, bias=nmx[:], accum_out=exs[:]).then_inc(s_ex, 1)
                    nc.scalar.activation(ex0[:], nmx[:], ACT.Exp).then_inc(s_ex, 1)

            step(0, None)
            with act.Fori(0, NG - 1) as i:
                step(i + 1, i)
            step(None, NG - 1)
            act.wait_ge(s_gap, NG)
            nc.scalar.activation(e2[:], gap[:], ACT.Exp, scale=-1.0).then_inc(s_e2, 1)

            def high(j, k):
                act.wait_ge(s_xt, j + 1)
                nc.scalar.activation(xh[:, k % 2, :], pb[k % 2][:, 0:P], ACT.Copy).then_inc(s_xh, 1)

            def silu(j, k):
                act.wait_ge(s_gu, j + 1)
                nc.scalar.activation(gate[:, k % 2, :], pb[2 + k % 2][:, 0:F], ACT.Silu).then_inc(s_silu, 1)

            def hidden_out(j, k):
                act.wait_ge(s_ht, j + 1)
                nc.scalar.activation(hidt[:, k % 2, :], pb[4 + k % 2][:, 0:F], ACT.Copy).then_inc(s_hc, 1)

            def tile_out(j, k, turn):
                act.wait_ge(s_dn, j + 1)
                if k == 0:
                    at_least(act, s_stA, 16 * turn)
                if k == HALF:
                    at_least(act, s_stB, 16 * turn)
                nc.scalar.activation(ye[:, k, :], pb[6 + k % 2][:, 0:D], ACT.Copy).then_inc(s_ye, 1)

            def tile_step(j, k, turn, last=False):
                if not (last and k + 1 >= STEP):
                    hidden_out(j + 1, k + 1)
                if not (last and k + AHEAD + 1 >= STEP):
                    high(j + AHEAD + 1, k + AHEAD + 1)
                if not (last and k + AHEAD >= STEP):
                    silu(j + AHEAD, k + AHEAD)
                tile_out(j, k, turn)

            high(0, 0)
            high(1, 1)
            silu(0, 0)
            high(2, 2)
            silu(1, 1)
            hidden_out(0, 0)
            high(3, 3)
            silu(2, 2)
            for k in range(STEP):
                tile_step(k, k, 0)
            with act.Fori(1, TURNS - 1) as turn:
                for k in range(STEP):
                    tile_step(turn * STEP + k, k, turn)
            for k in range(STEP):
                tile_step((TURNS - 1) * STEP + k, k, TURNS - 1, last=True)

        @block.vector
        def _(dve):
            V = nc.vector
            V.memset(eps[:], EPS).then_inc(s_const, 1)
            V.memset(ones[:], 1.0).then_inc(s_const, 1)
            dve.wait_ge(s_wa, 16 * N_ATT)
            V.tensor_copy(tri[:], tri_f[:]).then_inc(s_const, 1)
            V.tensor_tensor(fold[:, :], ident[:, 0:M], ident[:, M:2 * M], ALU.add).then_inc(s_const, 1)
            V.tensor_tensor(fqk[:], fq[:], fk[:], ALU.mult).then_inc(s_fqk, 1)
            V.tensor_scalar(bqkv[:], bqkv[:], float(S), None, ALU.mult).then_inc(s_fqk, 1)
            dve.wait_ge(s_const, 4)
            dve.wait_ge(s_fqk, 2)

            def wide(v, n):
                return v.unsqueeze(2).broadcast_to([v.shape[0], v.shape[1], n])

            def every(v, n):
                return v.unsqueeze(1).broadcast_to([v.shape[0], n, v.shape[1]])

            def row(buf, k):
                return buf[:, bass.ds(k, 1), :].rearrange("p a d -> p (a d)")

            def hold(sem_, n):
                dve.wait_ge(sem_, n)
                dve.sem_inc(s_held, 1)

            def moments(st, mean, dif, m2, sq, var_, s_half, s_sq, s_var_, n):
                V.tensor_tensor(mean, st[:, :, 1], st[:, :, 4], ALU.add).then_inc(s_half, 1)
                V.tensor_tensor(dif, st[:, :, 1], st[:, :, 4], ALU.subtract).then_inc(s_half, 1)
                V.tensor_tensor(m2, st[:, :, 2], st[:, :, 5], ALU.add).then_inc(s_half, 1)
                dve.wait_ge(s_half, 3 * n)
                V.scalar_tensor_tensor(sq, dif, D / 4.0, dif, ALU.mult, ALU.mult).then_inc(s_sq, 1)
                dve.wait_ge(s_sq, n)
                V.tensor_tensor(var_, sq, m2, ALU.add).then_inc(s_var_, 1)

            def step(f, b):
                if b is not None:
                    dve.wait_ge(s_zp, b + 1)
                    V.tensor_tensor(zs[:], pb[4][:, SEQS * P:2 * SEQS * P].rearrange("p (s d) -> p s d", d=D),
                                    every(bout[:], SEQS), ALU.add).then_inc(s_zs, 1)
                if f is not None:
                    hold(s_x, 16 * (f + 1))
                    for t in range(TG):
                        V.bn_stats(st1[:, t, :], row(x, f * TG + t)).then_inc(s_st1, 1)
                    dve.wait_ge(s_st1, TG * (f + 1))
                    moments(st1, mean1[:], dif1[:], m2_1[:], sq1[:], var1[:], s_half1, s_sq1, s_var1, f + 1)
                if b is not None:
                    dve.wait_ge(s_y, b + 1)
                    for t in range(TG):
                        V.bn_stats(st2[:, t, :], pb[5 + t // TS][:, t % TS * P:(t % TS + 1) * P]).then_inc(s_st2, 1)
                if f is not None:
                    dve.wait_ge(s_sd1, f + 1)
                    V.reciprocal(r1[:], sd1[:]).then_inc(s_r1, 1)
                if b is not None:
                    dve.wait_ge(s_st2, TG * (b + 1))
                    moments(st2, mean2[:], dif2[:], m2_2[:], sq2[:], var2[:], s_half2, s_sq2, s_var2, b + 1)
                if f is not None:
                    dve.wait_ge(s_r1, f + 1)
                    V.scalar_tensor_tensor(nm1[:], mean1[:], -0.5, r1[:], ALU.mult, ALU.mult).then_inc(s_nm1, 1)
                if b is not None:
                    dve.wait_ge(s_sd2, b + 1)
                    V.reciprocal(r2[:], sd2[:]).then_inc(s_r2, 1)
                    dve.wait_ge(s_r2, b + 1)
                    V.scalar_tensor_tensor(shift2[:, bass.ds(b * TG, TG)], mean2[:], -0.5, r2[:],
                                           ALU.mult, ALU.mult)
                    for t in range(TG):
                        V.scalar_tensor_tensor(row(x, b * TG + t), pb[5 + t // TS][:, t % TS * P:(t % TS + 1) * P],
                                               r2[:, t:t + 1], row(x, b * TG + t), ALU.mult, ALU.add).then_inc(s_x1, 1)
                    hold(s_x1, TG * (b + 1))
                    for t in range(TG):
                        V.bn_stats(st3[:, t, :], row(x, b * TG + t)).then_inc(s_st3, 1)
                    dve.wait_ge(s_st3, TG * (b + 1))
                    moments(st3, mean3[:], dif3[:], m2_3[:], sq3[:], var3[:], s_half3, s_sq3, s_var3, b + 1)
                if f is not None:
                    for q in range(SEQS):
                        dve.wait_ge(s_qkvp, SEQS * f + q + 1)
                        V.tensor_tensor(qkv[:, q, :], pb[1 + q][:, 0:3 * D], bqkv[:], ALU.add).then_inc(s_qkv, 1)
                if b is not None:
                    dve.wait_ge(s_sd3, b + 1)
                    V.reciprocal(r3[:], sd3[:]).then_inc(s_r3, 1)
                if f is not None:
                    dve.wait_ge(s_qkv, SEQS * (f + 1))
                    V.tensor_tensor(prod[:], qkv[:, :, 0:D], qkv[:, :, D:2 * D], ALU.mult).then_inc(s_prod, 1)
                if b is not None:
                    dve.wait_ge(s_r3, b + 1)
                    V.scalar_tensor_tensor(nm3[:], mean3[:], -0.5, r3[:], ALU.mult, ALU.mult).then_inc(s_nm3, 1)
                if f is not None:
                    dve.wait_ge(s_prod, f + 1)
                    V.tensor_tensor(prodw[:], prod[:], every(fqk[:], SEQS), ALU.mult).then_inc(s_prodw, 1)
                    V.tensor_tensor(vw[:], qkv[:, :, 2 * D:3 * D], every(fv[:], SEQS), ALU.mult).then_inc(s_vw, 1)
                    dve.wait_ge(s_prodw, f + 1)
                    V.tensor_reduce(red[:], prodw[:].rearrange("p s (h e) -> p (s h) e", e=HD), AX.X,
                                    ALU.add).then_inc(s_red, 1)
                    dve.wait_ge(s_sc, f + 1)
                    V.tensor_reduce(mx[:], pb[3][0:NH, 0:M], AX.X, ALU.max).then_inc(s_mx, 1)
                    dve.wait_ge(s_mx, f + 1)
                    V.tensor_scalar(nmx[:], mx[:], 0.0, -1.0, ALU.max, ALU.mult).then_inc(s_nmx, 1)
                if b is not None:
                    top2(b)
                if f is not None:
                    dve.wait_ge(s_ex, 2 * (f + 1))
                    V.scalar_tensor_tensor(tot[:], ex0[:], CUT, exs[:], ALU.mult, ALU.add).then_inc(s_tot, 1)
                    dve.wait_ge(s_tot, f + 1)
                    V.reciprocal(rtot[:], tot[:]).then_inc(s_rtot, 1)
                    dve.wait_ge(s_rtot, f + 1)
                    V.tensor_scalar(attn[:], every(ex[:], 2), rtot[:, 0:1], None, ALU.mult).then_inc(s_attn, 1)
                if b is not None:
                    counts(b)
                if f is not None:
                    dve.wait_ge(s_at, f + 1)
                    dve.wait_ge(s_vw, f + 1)
                    V.tensor_tensor(of[:].rearrange("p s (h e) -> p (s h) e", e=HD),
                                    vw[:].rearrange("p s (h e) -> p (s h) e", e=HD),
                                    wide(pb[3][:, M:M + NH], HD), ALU.mult).then_inc(s_of, 1)
                if b is not None:
                    route(b)

            logits = pb[7][:, 0:TG * E].rearrange("p (t e) -> p t e", e=E)
            prefix = pb[7][:, 64:64 + TG * E].rearrange("p (e t) -> p e t", t=TG)
            totals = pb[7][:, 128:128 + TG * E]

            def top2(b):
                dve.wait_ge(s_lg, b + 1)
                n = [TOP * b]

                def then(ins):
                    ins.then_inc(s_top, 1)
                    n[0] = n[0] + 1
                    dve.wait_ge(s_top, n[0])

                then(V.tensor_reduce(m1[:], logits, AX.X, ALU.max))
                then(V.tensor_tensor(eq[:], logits, wide(m1[:], E), ALU.is_equal))
                then(V.tensor_tensor(eqd[:], eq[:], every(e_down, TG), ALU.mult))
                then(V.tensor_reduce(i1[:], eqd[:], AX.X, ALU.max))
                then(V.tensor_tensor(oh1[:], every(e_down, TG), wide(i1[:], E), ALU.is_equal))
                then(V.scalar_tensor_tensor(rest[:], oh1[:], -BIG, logits, ALU.mult, ALU.add))
                then(V.tensor_reduce(m2[:], rest[:], AX.X, ALU.max))
                then(V.tensor_tensor(eq[:], rest[:], wide(m2[:], E), ALU.is_equal))
                then(V.tensor_tensor(eqd[:], eq[:], every(e_down, TG), ALU.mult))
                then(V.tensor_reduce(i2[:], eqd[:], AX.X, ALU.max))
                then(V.tensor_tensor(oh2[:], every(e_down, TG), wide(i2[:], E), ALU.is_equal))
                V.tensor_tensor(gap[:, bass.ds(b * TG, TG)], m1[:], m2[:], ALU.subtract).then_inc(s_gap, 1)

            def counts(b):
                V.tensor_tensor(cnt[:].rearrange("p e t -> p t e"), oh1[:], oh2[:], ALU.add).then_inc(s_cnt, 1)

            def route(b):
                n = [RT * b]

                def then(ins):
                    ins.then_inc(s_rt, 1)
                    n[0] = n[0] + 1
                    dve.wait_ge(s_rt, n[0])

                dve.wait_ge(s_pfx, b + 1)
                then(V.tensor_tensor_scan(inc[:].rearrange("p e t -> p (e t)"), t_keep, totals, 0.0, ALU.mult, ALU.add))
                then(V.tensor_scalar(up[:], inc[:, :, TG - 1], float(P - 1), None, ALU.add))
                then(V.tensor_scalar(tiles[:], up[:], 7, None, ALU.arith_shift_right))
                then(V.tensor_tensor_scan(cum[:], ones[:, 0:E], tiles[:], 0.0, ALU.mult, ALU.add))
                then(V.tensor_tensor(base[:], cum[:], tiles[:], ALU.subtract))
                then(V.tensor_tensor(pos[:], inc[:], totals.rearrange("p (e t) -> p e t", t=TG), ALU.subtract))
                then(V.tensor_tensor(pos2[:], pos[:], prefix, ALU.add))
                then(V.scalar_tensor_tensor(slot[:], wide(base[:], TG), float(P), pos2[:], ALU.mult, ALU.add))
                by_tile = slot[:].rearrange("p e t -> p t e")
                then(V.tensor_tensor(pick1[:], oh1[:], by_tile, ALU.mult))
                V.tensor_reduce(slots[:, bass.ds(b, 1), 0, :].rearrange("p a t -> p (a t)"), pick1[:], AX.X,
                                ALU.add).then_inc(s_slots, 1)
                then(V.tensor_tensor(pick2[:], oh2[:], by_tile, ALU.mult))
                V.tensor_reduce(slots[:, bass.ds(b, 1), 1, :].rearrange("p a t -> p (a t)"), pick2[:], AX.X,
                                ALU.add).then_inc(s_slots, 1)
                then(V.tensor_tensor(before[:].rearrange("p (j e) -> p j e", e=7), every(cum[0:1, 0:7], TPG * ROW),
                                     j_row[0:1].rearrange("p (j e) -> p j e", e=7), ALU.is_le))
                V.tensor_reduce(expert[:], before[:].rearrange("p (j e) -> p j e", e=7), AX.X, ALU.add).then_inc(s_cols, 1)
                dve.wait_ge(s_cols, 2 * b + 1)
                V.tensor_scalar(columns[:, bass.ds(b * TPG * ROW, TPG * ROW)], expert[:], float(2 * F), None,
                                ALU.mult).then_inc(s_cols, 1)

            step(0, None)
            dve.wait_ge(s_we, 16 * N_EXP)
            V.tensor_copy(w13h[:], w13[:]).then_inc(s_w13, 1)
            dve.wait_ge(s_w13, 1)
            V.tensor_tensor(w13l[:], w13[:], w13h[:].bitcast(F32), ALU.subtract).then_inc(s_w13, 1)
            with dve.Fori(0, NG - 1) as i:
                step(i + 1, i)
            step(None, NG - 1)
            dve.wait_ge(s_e2, 1)
            V.tensor_scalar(e2p[:], e2[:], 1.0, None, ALU.add).then_inc(s_wt, 1)
            dve.wait_ge(s_wt, 1)
            V.reciprocal(wt1[:], e2p[:]).then_inc(s_wt, 1)
            dve.wait_ge(s_wt, 2)
            V.tensor_tensor(wt2[:], wt1[:], e2[:], ALU.mult).then_inc(s_wt, 1)
            dve.wait_ge(s_wt, 3)

            def low(j, k):
                dve.wait_ge(s_xh, j + 1)
                V.tensor_tensor(xl[:, k % 2, :], pb[k % 2][:, 0:P], xh[:, k % 2, :].bitcast(F32),
                                ALU.subtract).then_inc(s_xl, 1)

            def hidden(j, k):
                dve.wait_ge(s_silu, j + 1)
                V.tensor_tensor(hid[:, k % 2, :], pb[2 + k % 2][:, F:2 * F], gate[:, k % 2, :],
                                ALU.mult).then_inc(s_h, 1)

            def tile_step(j, k, last=False):
                if not (last and k + AHEAD + 1 >= STEP):
                    low(j + AHEAD + 1, k + AHEAD + 1)
                if not (last and k + AHEAD >= STEP):
                    hidden(j + AHEAD, k + AHEAD)

            def pair_sum(k, slot_, odd, later=None):
                dve.wait_ge(s_gat[odd], (k >> 1) * 32 + 32)
                V.tensor_scalar(row(za, slot_), row(ya, slot_), wt1[:, bass.ds(k, 1)], None, ALU.mult).then_inc(s_za, 1)
                dve.wait_ge(s_za, k + 1)
                V.scalar_tensor_tensor(row(za, slot_), row(yb, slot_), wt2[:, bass.ds(k, 1)], row(za, slot_),
                                       ALU.mult, ALU.add).then_inc(s_z, 1)
                hold(s_z, k + 1)
                V.bn_stats(row(stz, k), row(za, slot_)).then_inc(s_stz, 1)

            def variances(g):
                part = slice(g * TG, (g + 1) * TG)
                dve.wait_ge(s_stz, TG * (g + 1))
                moments(stz[:, part, :], meanz[:, part], difz[:, part], m2_z[:, part], sqz[:, part],
                        varz[:, part], s_halfz, s_sqz, s_sumz, g + 1)
                dve.wait_ge(s_sumz, g + 1)
                V.tensor_scalar(var[:, part], varz[:, part], 1.0 / D, EPS, ALU.mult, ALU.add).then_inc(s_var, 1)

            def shifts(g):
                part = slice(g * TG, (g + 1) * TG)
                dve.wait_ge(s_rz, g + 1)
                V.scalar_tensor_tensor(cz[:, part], meanz[:, part], -0.5, rz[:, part], ALU.mult,
                                       ALU.mult).then_inc(s_cz, 1)
                dve.wait_ge(s_cz, 2 * g + 1)
                V.tensor_tensor(shift[:, part], cz[:, part], shift2[:, part], ALU.add).then_inc(s_cz, 1)
                dve.wait_ge(s_cz, 2 * g + 2)

            def final(k, slot_):
                V.scalar_tensor_tensor(row(zn, k), row(za, slot_), rz[:, bass.ds(k, 1)], row(x, k), ALU.mult,
                                       ALU.add).then_inc(s_zn, 1)
                dve.wait_ge(s_zn, k + 1)
                V.tensor_scalar(row(x, k), row(zn, k), shift[:, bass.ds(k, 1)], None, ALU.add).then_inc(s_out, 1)

            def wrap(k):
                return k % (2 * TG) if isinstance(k, int) else k & (2 * TG - 1)

            def turn_of(turn, sums, finals, last=False):
                for k in range(STEP):
                    tile_step(turn * STEP + k, k, last)
                    if k % 3 == 1 and sums:
                        kk = (turn - ZLAG) * ZT + k // 3
                        pair_sum(kk, wrap(kk), k // 3)
                    if k % 3 == 2 and finals:
                        kk = (turn - NLAG) * ZT + k // 3
                        final(kk, wrap(kk))

            low(0, 0)
            low(1, 1)
            hidden(0, 0)
            low(2, 2)
            hidden(1, 1)
            low(3, 3)
            hidden(2, 2)
            turn_of(0, False, False)
            with dve.Fori(1, ZLAG) as turn:
                turn_of(turn, False, False)
            with dve.Fori(ZLAG, NLAG) as turn:
                turn_of(turn, True, False)
            variances(0)
            for g in range(1, NG):
                first = NLAG + (g - 1) * TPG
                if first >= TURNS:
                    break
                end = min(first + TPG, TURNS - 1)
                turn_of(first, True, False)
                shifts(g - 1)
                for h in range(ZT):
                    final((first - NLAG) * ZT + h, wrap((first - NLAG) * ZT + h))
                with dve.Fori(first + 1, end) as turn:
                    turn_of(turn, True, True)
                if end < first + TPG:
                    turn_of(TURNS - 1, True, True, last=True)
                else:
                    variances(g)
            summed = (TURNS - ZLAG) * ZT
            normed = (TURNS - NLAG) * ZT
            for g in range(normed // TG, NG):
                for k in range(summed, (g + 1) * TG):
                    pair_sum(k, wrap(k), k % 2)
                if summed < (g + 1) * TG:
                    variances(g)
                    summed = (g + 1) * TG
                if normed == g * TG:
                    shifts(g)
                for k in range(normed, (g + 1) * TG):
                    final(k, wrap(k))
                normed = (g + 1) * TG

        @block.tensor
        def _(pe):
            T = nc.tensor
            pe.wait_ge(s_wa, 16 * N_ATT)
            pe.wait_ge(s_const, 4)

            def step(f, b):
                if b is not None:
                    pe.wait_ge(s_of, b + 1)
                    for q in range(SEQS):
                        ins = T.transpose(pb[4][:, q * P:(q + 1) * P], of[:, q, :], ident[:])
                    ins.then_inc(s_oftp, 1)
                    pe.wait_ge(s_oft, b + 1)
                    for q in range(SEQS):
                        ins = T.matmul(pb[4][:, (SEQS + q) * P:(SEQS + q + 1) * P], oft[:, q, :], wout[:],
                                       start=True, stop=True)
                    ins.then_inc(s_zp, 1)
                if b is not None:
                    pe.wait_ge(s_zs, b + 1)
                    for q in range(SEQS):
                        for t in range(TS):
                            ins = T.matmul(pb[5 + q][:, t * P:(t + 1) * P], ginv[:, t * P:(t + 1) * P], zs[:, q, :],
                                           start=True, stop=True)
                    ins.then_inc(s_y, 1)
                if f is not None:
                    pe.wait_ge(s_xn, TG * (f + 1))
                    for q in range(SEQS):
                        for t in range(TS):
                            ins = T.matmul(pb[0][:, q * P:(q + 1) * P], xn[:, q * TS + t, :], ftab[:, t, :],
                                           start=(t == 0), stop=(t == TS - 1))
                    ins.then_inc(s_dft, 1)
                if f is not None:
                    pe.wait_ge(s_xft, f + 1)
                    for q in range(SEQS):
                        T.matmul(pb[1 + q][:, 0:3 * D], xft[:, q, :], wqkv[:], start=True, stop=True).then_inc(s_qkvp, 1)
                    pe.wait_ge(s_red, f + 1)
                    T.matmul(pb[3][0:NH, 0:M], red[:], fold[:], start=True, stop=True).then_inc(s_sc, 1)
                if b is not None:
                    pe.wait_ge(s_xn2, TG * (b + 1))
                    for q in range(SEQS):
                        for t in range(TS):
                            ins = T.transpose(pb[5 + q][:, t * P:(t + 1) * P], xn2[:, q * TS + t, :], ident[:])
                        ins.then_inc(s_xn2p, 1)
                    pe.wait_ge(s_xn2t, SEQS * (b + 1))
                    for t in range(TG):
                        ins = T.matmul(pb[7][:, t * E:(t + 1) * E], xn2t[:, t // TS, t % TS * P:(t % TS + 1) * P], rw[:],
                                       start=True, stop=True)
                    ins.then_inc(s_lg, 1)
                if f is not None:
                    pe.wait_ge(s_attn, f + 1)
                    T.matmul(pb[3][:, M:M + NH], attn[:].rearrange("h a m -> h (a m)"), ident[0:NH, 0:NH],
                             start=True, stop=True).then_inc(s_at, 1)
                if b is not None:
                    pe.wait_ge(s_cnt, b + 1)
                    flat = cnt[:].rearrange("p e t -> p (e t)")
                    T.matmul(pb[7][:, 64:128], tri[:], flat, start=True, stop=True)
                    T.matmul(pb[7][:, 128:192], ones[:], flat, start=True, stop=True).then_inc(s_pfx, 1)

            step(0, None)
            with pe.Fori(0, NG - 1) as i:
                step(i + 1, i)
            step(None, NG - 1)
            pe.wait_ge(s_cols, 2 * NG)
            pe.wait_ge(s_slots, 2 * NG)
            pe.wait_ge(s_w13, 2)
            pe.wait_ge(s_we, 16 * N_EXP)

            def turned(j, k, turn):
                if k % STEP == 0:
                    pe.wait_ge(s_xeA, 16 * (turn + 1))
                if k % STEP == HALF:
                    pe.wait_ge(s_xeB, 16 * (turn + 1))
                T.transpose(pb[k % 2][:, 0:P], xe[:, k % STEP, :], ident[:]).then_inc(s_xt, 1)

            cols = [pe.alloc_register(f"columns_{k}") for k in range(STEP + AHEAD)]

            def experts_of(turn, n, first=0):
                pe.load(cols[first:first + n], columns[0:1, bass.ds(turn * ROW, n)])
                return [pe.snap(r, min_val=0, max_val=(E - 1) * 2 * F) for r in cols[first:first + n]]

            def gate_up(j, k, col):
                pe.wait_ge(s_xl, j + 1)
                out_, c = pb[2 + k % 2][:], k % 2
                hi, lo = w13h[:, bass.ds(col, 2 * F)], w13l[:, bass.ds(col, 2 * F)]
                T.matmul(out_, xh[:, c, :], hi, start=True, stop=False)
                T.matmul(out_, xh[:, c, :], lo, start=False, stop=False)
                T.matmul(out_, xl[:, c, :], hi, start=False, stop=True).then_inc(s_gu, 1)

            def hidden_turned(j, k):
                pe.wait_ge(s_h, j + 1)
                for c in range(FC):
                    ins = T.transpose(pb[4 + k % 2][:, c * P:(c + 1) * P], hid[:, k % 2, c * P:(c + 1) * P], ident[:])
                ins.then_inc(s_ht, 1)

            def down(j, k, col):
                pe.wait_ge(s_hc, j + 1)
                for c in range(FC):
                    ins = T.matmul(pb[6 + k % 2][:, 0:D], hidt[:, k % 2, c * P:(c + 1) * P],
                                   w2[:, bass.ds(col + c * D, D)], start=(c == 0), stop=(c == FC - 1))
                ins.then_inc(s_dn, 1)

            def tile_step(j, k, turn, exp, last=False):
                if not (last and k + 1 >= STEP):
                    hidden_turned(j + 1, k + 1)
                if not (last and k + AHEAD + 1 >= STEP):
                    turned(j + AHEAD + 1, k + AHEAD + 1, turn + (k + AHEAD + 1) // STEP)
                if not (last and k + AHEAD >= STEP):
                    gate_up(j + AHEAD, k + AHEAD, exp[k + AHEAD])
                down(j, k, exp[k])

            exp = experts_of(0, STEP)
            turned(0, 0, 0)
            turned(1, 1, 0)
            gate_up(0, 0, exp[0])
            turned(2, 2, 0)
            gate_up(1, 1, exp[1])
            hidden_turned(0, 0)
            turned(3, 3, 0)
            gate_up(2, 2, exp[2])
            exp += experts_of(1, AHEAD, STEP)
            for k in range(STEP):
                tile_step(k, k, 0, exp)
            with pe.Fori(1, TURNS - 1) as turn:
                exp = experts_of(turn, STEP) + experts_of(turn + 1, AHEAD, STEP)
                for k in range(STEP):
                    tile_step(turn * STEP + k, k, turn, exp)
            exp = experts_of(TURNS - 1, STEP)
            for k in range(STEP):
                tile_step((TURNS - 1) * STEP + k, k, TURNS - 1, exp, last=True)


def kernel(L0_attn_query, L0_attn_w_qkv, L0_attn_b_qkv, L0_attn_w_out, L0_attn_b_out, L0_attn_freq_q,
           L0_attn_freq_k, L0_attn_freq_v, L0_ffn_router_w, L0_ffn_w1, L0_ffn_w3, L0_ffn_w2):
    import concourse.bacc as bacc
    from concourse.bass_utils import run_bass_kernel_spmd

    f32 = np.float32

    def both_halves(w):
        w = np.transpose(np.asarray(w), (1, 0, 2)).reshape(M, D)
        return np.concatenate([w, w], axis=0)

    def first_row(b):
        b = np.asarray(b)
        return np.concatenate([b[None], np.zeros((P - 1, b.shape[0]), b.dtype)], axis=0)

    angle = 2 * np.pi * (np.outer(np.arange(S), np.arange(M)) % S) / S
    ftab = np.concatenate([np.cos(angle), np.sin(angle)], axis=1).astype(f32)
    rows = np.concatenate([
        8 - np.arange(E),
        np.tile((np.arange(TG) > 0).astype(f32), E),
        np.repeat((np.arange(TPG)[:, None] * STEP + np.arange(ROW)).ravel(), 7)]).astype(f32)
    w1, w3, w2 = (np.asarray(w) for w in (L0_ffn_w1, L0_ffn_w3, L0_ffn_w2))
    arrays = {
        "query": np.asarray(L0_attn_query).reshape(B * S, D),
        "w_qkv": np.asarray(L0_attn_w_qkv).T,
        "b_qkv": first_row(L0_attn_b_qkv),
        "w_out": np.asarray(L0_attn_w_out).T,
        "b_out": first_row(L0_attn_b_out),
        "freq_q": both_halves(L0_attn_freq_q),
        "freq_k": both_halves(L0_attn_freq_k),
        "freq_v": both_halves(L0_attn_freq_v),
        "router_w": np.asarray(L0_ffn_router_w),
        "w13": np.concatenate([w1, w3], axis=2).transpose(1, 0, 2).reshape(D, E * 2 * F),
        "w2": w2.reshape(E, FC, P, D).transpose(2, 0, 1, 3).reshape(P, E * FC * D),
        "dft": ftab,
        "dft_t": ftab.T,
        "ident": np.eye(P, dtype=f32),
        "tri": np.triu(np.ones((P, P), f32), 1),
        "rows": np.tile(rows[None], (P, 1)),
    }
    nc = bacc.Bacc("TRN2", target_bir_lowering=False, num_devices=1)
    ins, args = {}, []
    for name, a in arrays.items():
        ins[f"in_{name}"] = np.ascontiguousarray(a)
        args.append(nc.dram_tensor(f"in_{name}", a.shape, mybir.dt.from_np(a.dtype), kind="ExternalInput").ap())
    out = nc.dram_tensor("out_x", (B * S, D), F32, kind="ExternalOutput").ap()
    build(nc, *args, out)
    r = run_bass_kernel_spmd(nc, [ins], core_ids=[0])
    return r.results[0]["out_x"].reshape(B, S, D)
```

```python
from contextlib import ExitStack

import numpy as np

import concourse.bass as bass
from concourse import mybir

ALU = mybir.AluOpType
ACT = mybir.ActivationFunctionType
AX = mybir.AxisListType
F32 = mybir.dt.float32
F32R = mybir.dt.float32r
BF16 = mybir.dt.bfloat16
I32 = mybir.dt.int32

P = 128
B, S, D = 8, 512, 128
H, M, HD = 16, 64, 8
E, F = 8, 256
FC = F // P
EPS = 1e-5
CUT = float(S - M)

TS = S // P
SEQS = 2
NG = B // SEQS
TG = TS * SEQS
NT = NG * TG
STEP = 6
ET = 24
TURNS = NG * ET // STEP
TPG = ET // STEP
ROW = 8
AHEAD = 3
SLOTS = ET * P
HALF = STEP // 2
ZLAG = TPG + 1
NLAG = ZLAG + TPG
ZT = TG // TPG
BIG = 3.0e38

assert SEQS * TS * P * 2 // P + E - 1 <= ET and ET % STEP == 0 and STEP % 2 == 0


def at_least(eng, sem, n):
    if isinstance(n, int) and n <= 0:
        return
    eng.wait_ge(sem, n)


def parts(widths):
    at, n = {}, 0
    for name, w in widths:
        at[name] = slice(n, n + w)
        n += w
    return at, n


FRONT, N_FRONT = parts([("ftab", TS * P), ("wqkv", 3 * D), ("ident", P), ("fq", D), ("fk", D), ("fv", D)])
BACK, N_BACK = parts([("ginv", S), ("wout", D), ("rw", E), ("tri", P), ("down", E), ("keep", E * TG),
                      ("tile", TPG * ROW * (E - 1))])
BIAS, N_BIAS = parts([("bqkv", 3 * D), ("bout", D)])


def build(nc, x_in, front_in, back_in, bias_in, w13_in, w2_in, out):
    with ExitStack() as ctx:
        ctx.enter_context(nc.allow_low_precision(reason="sums of small whole numbers, kept as integers"))

        def sb(name, shape, dt=F32):
            return ctx.enter_context(nc.sbuf_tensor(name, shape, dt))

        def bank(name):
            return ctx.enter_context(nc.psum_tensor(name, [P, 512], F32))

        def sem(name):
            return ctx.enter_context(nc.semaphore(name))

        front = sb("front", [P, N_FRONT])
        ftab = front[:, FRONT["ftab"]].rearrange("p (t f) -> p t f", t=TS)
        wqkv = front[:, FRONT["wqkv"]]
        ident = front[:, FRONT["ident"]]
        fq, fk, fv = front[:, FRONT["fq"]], front[:, FRONT["fk"]], front[:, FRONT["fv"]]
        back = sb("back", [P, N_BACK])
        ginv = back[:, BACK["ginv"]]
        wout = back[:, BACK["wout"]]
        rw = back[:, BACK["rw"]]
        tri_f = back[:, BACK["tri"]]
        e_down = back[:, BACK["down"]]
        t_keep = back[:, BACK["keep"]]
        j_row = back[:, BACK["tile"]]
        bias = sb("bias", [1, N_BIAS])
        bout = bias[:, BIAS["bout"]]
        bqkv = sb("bqkv", [1, 3 * D])
        tri = sb("tri", [P, P], BF16)
        ones = sb("ones", [P, P], BF16)
        fold = sb("fold", [P, M])
        eps = sb("eps", [P, 1])
        fqk = sb("fqk", [P, D])
        w13 = sb("w13", [P, E * 2 * F])
        w13h = sb("w13h", [P, E * 2 * F], F32R)
        w13l = sb("w13l", [P, E * 2 * F], F32R)
        w2 = sb("w2", [P, E * 2 * F])
        zero = sb("zero", [P, ET * P])

        x = sb("x", [P, NT, D])
        shift2 = sb("shift2", [P, NT])

        st1 = sb("st1", [P, TG, 6])
        mean1 = sb("mean1", [P, TG])
        dif1 = sb("dif1", [P, TG])
        m2_1 = sb("m2_1", [P, TG])
        sq1 = sb("sq1", [P, TG])
        var1 = sb("var1", [P, TG])
        sd1 = sb("sd1", [P, TG])
        r1 = sb("r1", [P, TG])
        nm1 = sb("nm1", [P, TG])
        xn = sb("xn", [P, TG, D])
        xft = sb("xft", [P, SEQS, P])
        qk = sb("qk", [P, SEQS, D])
        prod = sb("prod", [P, SEQS, D])
        prodw = sb("prodw", [P, SEQS, D])
        vw = sb("vw", [P, SEQS, D])
        red = sb("red", [P, SEQS * H])
        NH = SEQS * H
        mx = sb("mx", [NH, 1])
        nmx = sb("nmx", [NH, 1])
        ex = sb("ex", [NH, M])
        exs = sb("exs", [NH, 1])
        ex0 = sb("ex0", [NH, 1])
        tot = sb("tot", [NH, 1])
        rtot = sb("rtot", [NH, 1])
        attn = sb("attn", [NH, 2, M])
        of = sb("of", [P, SEQS, D])
        oft = sb("oft", [P, SEQS, P])
        zs = sb("zs", [P, SEQS, D])

        st2 = sb("st2", [P, TG, 6])
        mean2 = sb("mean2", [P, TG])
        dif2 = sb("dif2", [P, TG])
        m2_2 = sb("m2_2", [P, TG])
        sq2 = sb("sq2", [P, TG])
        var2 = sb("var2", [P, TG])
        sd2 = sb("sd2", [P, TG])
        r2 = sb("r2", [P, TG])
        st3 = sb("st3", [P, TG, 6])
        mean3 = sb("mean3", [P, TG])
        dif3 = sb("dif3", [P, TG])
        m2_3 = sb("m2_3", [P, TG])
        sq3 = sb("sq3", [P, TG])
        var3 = sb("var3", [P, TG])
        sd3 = sb("sd3", [P, TG])
        r3 = sb("r3", [P, TG])
        nm3 = sb("nm3", [P, TG])
        xn2 = sb("xn2", [P, TG, D])
        rows2 = sb("rows2", [P, NT, D])
        xn2t = sb("xn2t", [P, SEQS, S])

        m1 = sb("m1", [P, TG])
        m2 = sb("m2", [P, TG])
        i1 = sb("i1", [P, TG])
        i2 = sb("i2", [P, TG])
        eq = sb("eq", [P, TG, E])
        eqd = sb("eqd", [P, TG, E])
        oh1 = sb("oh1", [P, TG, E])
        oh2 = sb("oh2", [P, TG, E])
        rest = sb("rest", [P, TG, E])
        gap = sb("gap", [P, NT])
        e2 = sb("e2", [P, NT])
        e2p = sb("e2p", [P, NT])
        wt1 = sb("wt1", [P, NT])
        wt2 = sb("wt2", [P, NT])
        cnt = sb("cnt", [P, E, TG], BF16)
        inc = sb("inc", [P, E, TG])
        pos = sb("pos", [P, E, TG])
        pos2 = sb("pos2", [P, E, TG])
        up = sb("up", [P, E], I32)
        tiles = sb("tiles", [P, E], I32)
        cum = sb("cum", [P, E])
        base = sb("base", [P, E])
        slot = sb("slot", [P, E, TG])
        pick1 = sb("pick1", [P, TG, E])
        pick2 = sb("pick2", [P, TG, E])
        slots = sb("slots", [P, NG, 2, TG], I32)
        before = sb("before", [1, TPG * ROW * 7])
        expert = sb("expert", [1, TPG * ROW])
        columns = sb("columns", [1, TURNS * ROW], I32)

        xe = sb("xe", [P, STEP, D])
        xh = sb("xh", [P, 2, P], F32R)
        xl = sb("xl", [P, 2, P], F32R)
        gate = sb("gate", [P, 2, F])
        hid = sb("hid", [P, 2, F])
        hidt = sb("hidt", [P, 2, F])
        ye = sb("ye", [P, STEP, D])

        ya = sb("ya", [P, 2 * TG, D])
        yb = sb("yb", [P, 2 * TG, D])
        za = sb("za", [P, 2 * TG, D])
        stz = sb("stz", [P, NT, 6])
        meanz = sb("meanz", [P, NT])
        difz = sb("difz", [P, NT])
        m2_z = sb("m2_z", [P, NT])
        sqz = sb("sqz", [P, NT])
        varz = sb("varz", [P, NT])
        var = sb("var", [P, NT])
        rz = sb("rz", [P, NT])
        cz = sb("cz", [P, NT])
        shift = sb("shift", [P, NT])
        half = sb("half", [P, TG])
        zn = rows2

        pair = [ctx.enter_context(nc.psum_tensor(f"pair{i}", [P, 2, 512], F32)) for i in range(4)]
        pb = [pair[i // 2][:, i % 2, :] for i in range(8)]
        dft_, z_, small, of_t, route_ = pb[0][:, 0:SEQS * P], pb[0][:, SEQS * P:2 * SEQS * P], pb[1], pb[4], pb[5]
        qkv, y = pair[1], pair[3]

        xg = [nc.dram_tensor(f"xg{g}", [SLOTS, D], F32, kind="Internal").ap() for g in range(NG)]
        yg = [nc.dram_tensor(f"yg{g}", [SLOTS, D], F32, kind="Internal").ap() for g in range(NG)]

        s_held = sem("waits_passed")
        s_x = sem("x_loaded")
        s_front = sem("front_weights_loaded")
        s_back = sem("back_weights_loaded")
        s_bias = sem("biases_loaded")
        s_we = sem("expert_weights_loaded")
        s_const = sem("constants_ready")
        s_halves = sem("exponents_ready")
        s_fqk = sem("filters_multiplied")
        s_w13 = sem("w13_split")
        s_zero = sem("zero_tile_ready")
        s_xgz = sem("slots_zeroed")
        s_st1 = sem("stats1")
        s_half1 = sem("halves_joined1")
        s_sq1 = sem("difference_squared1")
        s_var1 = sem("variance1")
        s_sd1 = sem("deviation1")
        s_r1 = sem("reciprocal1")
        s_nm1 = sem("shift1_ready")
        s_xn = sem("xn_ready")
        s_dft = sem("dft_done")
        s_xft = sem("xft_copied")
        s_qkvp = sem("qkv_done")
        s_qk = sem("q_copied")
        s_prod = sem("qk_product")
        s_prodw = sem("qk_filtered")
        s_vw = sem("v_filtered")
        s_red = sem("qk_summed")
        s_sc = sem("scores_done")
        s_mx = sem("max_taken")
        s_nmx = sem("max_negated")
        s_ex = sem("exp_done")
        s_tot = sem("sum_done")
        s_rtot = sem("sum_inverted")
        s_attn = sem("attention_ready")
        s_at = sem("attention_turned")
        s_of = sem("of_ready")
        s_oftp = sem("of_turned")
        s_oft = sem("oft_copied")
        s_zp = sem("z_done")
        s_zs = sem("z_biased")
        s_y = sem("y_done")
        s_st2 = sem("stats2")
        s_half2 = sem("halves_joined2")
        s_sq2 = sem("difference_squared2")
        s_var2 = sem("variance2")
        s_sd2 = sem("deviation2")
        s_r2 = sem("reciprocal2")
        s_x1 = sem("x1_ready")
        s_st3 = sem("stats3")
        s_half3 = sem("halves_joined3")
        s_sq3 = sem("difference_squared3")
        s_var3 = sem("variance3")
        s_sd3 = sem("deviation3")
        s_r3 = sem("reciprocal3")
        s_nm3 = sem("shift3_ready")
        s_xn2 = sem("xn2_ready")
        s_rows = sem("rows_copied")
        s_xn2p = sem("xn2_turned")
        s_xn2t = sem("xn2t_copied")
        s_lg = sem("logits_done")
        s_top = sem("top2_steps")
        s_cnt = sem("counts_ready")
        s_pfx = sem("prefix_done")
        s_rt = sem("route_steps")
        s_slots = sem("slots_ready")
        s_cols = sem("columns_ready")
        s_scat = [sem(f"rows_scattered_{g}") for g in range(NG)]
        s_gap = sem("gaps_ready")
        s_e2 = sem("gap_exp")
        s_wt = sem("weights_of_pairs")
        s_xeA = sem("rows_loaded_a")
        s_xeB = sem("rows_loaded_b")
        s_xt = sem("tile_turned")
        s_xh = sem("tile_high")
        s_xl = sem("tile_low")
        s_gu = sem("gate_up_done")
        s_silu = sem("silu_done")
        s_h = sem("hidden_ready")
        s_ht = sem("hidden_turned")
        s_hc = sem("hidden_copied")
        s_dn = sem("down_done")
        s_ye = sem("tile_out")
        s_stA = sem("tiles_stored_a")
        s_stB = sem("tiles_stored_b")
        s_gat = [sem("pair_gathered_even"), sem("pair_gathered_odd")]
        s_za = sem("first_weighted")
        s_z = sem("sum_ready")
        s_stz = sem("stats_z")
        s_halfz = sem("halves_joined_z")
        s_sqz = sem("difference_squared_z")
        s_sumz = sem("variance_summed_z")
        s_var = sem("variance_z")
        s_rz = sem("rsqrt_z")
        s_cz = sem("shift_z")
        s_zn = sem("z_scaled")
        s_out = sem("out_ready")
        s_stored = sem("out_stored")

        x_dram = x_in.rearrange("(g t p) d -> g p t d", p=P, t=TG)
        out_dram = out.rearrange("(k t p) d -> k p t d", p=P, t=TG // 2)
        N_EXP = 2
        TOP, RT = 11, 11

        block = ctx.enter_context(nc.Block())

        @block.sync
        def _(sp):
            for g in range(NG):
                at_least(sp, s_x, 16 * g)
                sp.dma_start(x[:, g * TG:(g + 1) * TG, :], x_dram[g]).then_inc(s_x, 16)
            sp.dma_start(w13[:], w13_in).then_inc(s_we, 16)
            sp.dma_start(w2[:].rearrange("p (e n) -> p e n", n=2 * F)[:, :, 0:FC * D],
                         w2_in.rearrange("p (e n) -> p e n", n=FC * D)).then_inc(s_we, 16)
            sp.wait_ge(s_zero, 1)
            for g in range(NG):
                sp.dma_start(xg[g].rearrange("(p j) d -> p (j d)", p=P), zero[:]).then_inc(s_xgz, 16)

            def tiles_of(dram, turn, half):
                g, r = turn // TPG, (turn % TPG * STEP + half * HALF) * P
                return dram[g][r:r + HALF * P, :].rearrange("(j p) d -> p j d", p=P)

            def load(turn, half):
                if turn % TPG == 0:
                    sp.wait_ge(s_scat[turn // TPG], 16 * 2 * TG)
                at_least(sp, s_xt, STEP * (turn - 1) + HALF * (half + 1))
                sp.dma_start(xe[:, half * HALF:(half + 1) * HALF, :], tiles_of(xg, turn, half)).then_inc(
                    (s_xeA, s_xeB)[half], 16)

            def store(turn, half):
                sp.wait_ge(s_ye, STEP * turn + HALF * (half + 1))
                sp.dma_start(tiles_of(yg, turn, half), ye[:, half * HALF:(half + 1) * HALF, :]).then_inc(
                    (s_stA, s_stB)[half], 16)

            def store_out(k):
                sp.wait_ge(s_out, (k + 1) * TG // 2)
                sp.dma_start(out_dram[k], x[:, k * TG // 2:(k + 1) * TG // 2, :]).then_inc(s_stored, 16)

            stored = 0
            load(0, 0)
            load(0, 1)
            for turn in range(TURNS):
                if turn < TURNS - 1:
                    load(turn + 1, 0)
                if turn:
                    store(turn - 1, 1)
                if turn < TURNS - 1:
                    load(turn + 1, 1)
                store(turn, 0)
                if turn >= NLAG + 2 and turn % 2 == 1:
                    store_out(stored)
                    stored += 1
            store(TURNS - 1, 1)
            while stored < 2 * NG:
                store_out(stored)
                stored += 1
            sp.wait_ge(s_stored, 16 * 2 * NG)

        @block.gpsimd
        def _(pool):
            nc.gpsimd.memset(zero[:], 0.0).then_inc(s_zero, 1)
            nc.gpsimd.memset(half[:], -0.5).then_inc(s_halves, 1)
            pool.wait_ge(s_we, 16 * N_EXP)
            nc.gpsimd.tensor_copy(w13h[:], w13[:]).then_inc(s_w13, 1)
            pool.wait_ge(s_w13, 1)
            nc.gpsimd.tensor_tensor(w13l[:], w13[:], w13h[:].bitcast(F32), ALU.subtract).then_inc(s_w13, 1)

            def copy_rows(g):
                pool.wait_ge(s_xn2, TG * (g + 1))
                nc.gpsimd.tensor_copy(rows2[:, g * TG:(g + 1) * TG, :], xn2[:]).then_inc(s_rows, 1)

            copy_rows(0)
            pool.wait_ge(s_xgz, 16 * NG)
            for g in range(NG):
                pool.wait_ge(s_slots, 2 * (g + 1))
                pool.wait_ge(s_rows, g + 1)
                for t in range(TG):
                    if t == TG // 2 and g + 1 < NG:
                        copy_rows(g + 1)
                    for k in range(2):
                        pool.indirect_dma_start(
                            out=xg[g], out_offset=bass.IndirectOffsetOnAxis(ap=slots[:, g, k, t:t + 1], axis=0),
                            in_=rows2[:, g * TG + t, :], in_offset=None).then_inc(s_scat[g], 16)
            pool.wait_ge(s_halves, 1)

            def inverse_deviations(g):
                pool.wait_ge(s_var, g + 1)
                nc.gpsimd.tensor_tensor(rz[:, g * TG:(g + 1) * TG], var[:, g * TG:(g + 1) * TG], half[:],
                                        ALU.pow).then_inc(s_rz, 1)

            for g in range(NG):
                pool.wait_ge(s_stA, 16 * TPG * (g + 1))
                pool.wait_ge(s_stB, 16 * TPG * (g + 1))
                for t in range(TG):
                    k = g * TG + t
                    at_least(pool, s_out, TG * (g - 1) if t == 0 else 0)
                    at_least(pool, s_gat[t % 2], 32 * (k // 2))
                    if g and t == TG // 2:
                        inverse_deviations(g - 1)
                    for i, y in enumerate((ya, yb)):
                        pool.indirect_dma_start(
                            out=y[:, k % (2 * TG), :], out_offset=None, in_=yg[g],
                            in_offset=bass.IndirectOffsetOnAxis(ap=slots[:, g, i, t:t + 1], axis=0),
                        ).then_inc(s_gat[t % 2], 16)
            inverse_deviations(NG - 1)

        @block.scalar
        def _(act):
            act.dma_start(front[:], front_in).then_inc(s_front, 16)
            act.dma_start(bias[:], bias_in).then_inc(s_bias, 16)
            act.dma_start(back[:], back_in).then_inc(s_back, 16)

            def step(f, m, b):
                if m is not None:
                    act.wait_ge(s_oftp, m + 1)
                    nc.scalar.activation(oft[:], of_t[:, 0:SEQS * P], ACT.Copy).then_inc(s_oft, 1)
                if b is not None:
                    act.wait_ge(s_nm3, b + 1)
                    if b_copied(b):
                        act.wait_ge(s_rows, b)
                    for t in range(TS):
                        norm3(b, t)
                if m is not None:
                    act.wait_ge(s_zp, m + 1)
                    nc.scalar.activation(zs[:], z_, ACT.Copy).then_inc(s_zs, 1)
                if f is not None:
                    act.wait_ge(s_var1, f + 1)
                    nc.scalar.activation(sd1[:], var1[:], ACT.Sqrt, bias=eps[:], scale=1.0 / D).then_inc(s_sd1, 1)
                if b is not None:
                    for t in range(TS, TG):
                        norm3(b, t)
                    for q in range(SEQS):
                        act.wait_ge(s_xn2p, SEQS * b + q + 1)
                        nc.scalar.activation(xn2t[:, q, :], qkv[:, q, :], ACT.Copy).then_inc(s_xn2t, 1)
                if f is not None:
                    act.wait_ge(s_nm1, f + 1)
                    for t in range(TG):
                        nc.scalar.activation(xn[:, t, :], x[:, bass.ds(f * TG + t, 1), :].rearrange("p a d -> p (a d)"),
                                             ACT.Identity, bias=nm1[:, t:t + 1], scale=r1[:, t:t + 1]).then_inc(s_xn, 1)
                if m is not None:
                    act.wait_ge(s_var2, m + 1)
                    nc.scalar.activation(sd2[:], var2[:], ACT.Sqrt, bias=eps[:], scale=1.0 / D).then_inc(s_sd2, 1)
                if f is not None:
                    act.wait_ge(s_dft, f + 1)
                    nc.scalar.activation(xft[:], dft_, ACT.Copy).then_inc(s_xft, 1)
                if m is not None:
                    act.wait_ge(s_var3, m + 1)
                    nc.scalar.activation(sd3[:], var3[:], ACT.Sqrt, bias=eps[:], scale=1.0 / D).then_inc(s_sd3, 1)
                if f is not None:
                    act.wait_ge(s_nmx, f + 1)
                    nc.scalar.activation(ex[:], small[0:NH, 0:M], ACT.Exp, bias=nmx[:], accum_out=exs[:]).then_inc(s_ex, 1)
                    nc.scalar.activation(ex0[:], nmx[:], ACT.Exp).then_inc(s_ex, 1)

            def norm3(b, t):
                nc.scalar.activation(xn2[:, t, :], x[:, bass.ds(b * TG + t, 1), :].rearrange("p a d -> p (a d)"),
                                     ACT.Identity, bias=nm3[:, t:t + 1], scale=r3[:, t:t + 1]).then_inc(s_xn2, 1)

            def b_copied(b):
                return not isinstance(b, int) or b > 0

            step(0, None, None)
            step(1, 0, None)
            step(2, 1, 0)
            with act.Fori(0, NG - 3) as i:
                step(i + 3, i + 2, i + 1)
            step(None, NG - 1, NG - 2)
            step(None, None, NG - 1)
            act.wait_ge(s_gap, NG)
            nc.scalar.activation(e2[:], gap[:], ACT.Exp, scale=-1.0).then_inc(s_e2, 1)

            def high(j, k):
                act.wait_ge(s_xt, j + 1)
                nc.scalar.activation(xh[:, k % 2, :], pb[k % 2][:, 0:P], ACT.Copy).then_inc(s_xh, 1)

            def silu(j, k):
                act.wait_ge(s_gu, j + 1)
                nc.scalar.activation(gate[:, k % 2, :], pb[2 + k % 2][:, 0:F], ACT.Silu).then_inc(s_silu, 1)

            def hidden_out(j, k):
                act.wait_ge(s_ht, j + 1)
                nc.scalar.activation(hidt[:, k % 2, :], pb[4 + k % 2][:, 0:F], ACT.Copy).then_inc(s_hc, 1)

            def tile_out(j, k, turn):
                act.wait_ge(s_dn, j + 1)
                if k == 0:
                    at_least(act, s_stA, 16 * turn)
                if k == HALF:
                    at_least(act, s_stB, 16 * turn)
                nc.scalar.activation(ye[:, k, :], pb[6 + k % 2][:, 0:D], ACT.Copy).then_inc(s_ye, 1)

            def tile_step(j, k, turn, last=False):
                if not (last and k + 1 >= STEP):
                    hidden_out(j + 1, k + 1)
                if not (last and k + AHEAD + 1 >= STEP):
                    high(j + AHEAD + 1, k + AHEAD + 1)
                if not (last and k + AHEAD >= STEP):
                    silu(j + AHEAD, k + AHEAD)
                tile_out(j, k, turn)

            high(0, 0)
            high(1, 1)
            silu(0, 0)
            high(2, 2)
            silu(1, 1)
            hidden_out(0, 0)
            high(3, 3)
            silu(2, 2)
            for k in range(STEP):
                tile_step(k, k, 0)
            with act.Fori(1, TURNS - 1) as turn:
                for k in range(STEP):
                    tile_step(turn * STEP + k, k, turn)
            for k in range(STEP):
                tile_step((TURNS - 1) * STEP + k, k, TURNS - 1, last=True)

        @block.vector
        def _(dve):
            V = nc.vector
            V.memset(eps[:], EPS).then_inc(s_const, 1)
            V.memset(ones[:], 1.0).then_inc(s_const, 1)

            def wide(v, n):
                return v.unsqueeze(2).broadcast_to([v.shape[0], v.shape[1], n])

            def every(v, n):
                return v.unsqueeze(1).broadcast_to([v.shape[0], n, v.shape[1]])

            def row(buf, k):
                return buf[:, bass.ds(k, 1), :].rearrange("p a d -> p (a d)")

            def hold(sem_, n):
                dve.wait_ge(sem_, n)
                dve.sem_inc(s_held, 1)

            def moments(st, mean, dif, m2, sq, var_, s_half, s_sq, s_var_, n):
                V.tensor_tensor(mean, st[:, :, 1], st[:, :, 4], ALU.add).then_inc(s_half, 1)
                V.tensor_tensor(dif, st[:, :, 1], st[:, :, 4], ALU.subtract).then_inc(s_half, 1)
                V.tensor_tensor(m2, st[:, :, 2], st[:, :, 5], ALU.add).then_inc(s_half, 1)
                dve.wait_ge(s_half, 3 * n)
                V.scalar_tensor_tensor(sq, dif, D / 4.0, dif, ALU.mult, ALU.mult).then_inc(s_sq, 1)
                dve.wait_ge(s_sq, n)
                V.tensor_tensor(var_, sq, m2, ALU.add).then_inc(s_var_, 1)

            def centre1(f):
                hold(s_x, 16 * (f + 1))
                for t in range(TG):
                    V.bn_stats(st1[:, t, :], row(x, f * TG + t)).then_inc(s_st1, 1)
                dve.wait_ge(s_st1, TG * (f + 1))
                moments(st1, mean1[:], dif1[:], m2_1[:], sq1[:], var1[:], s_half1, s_sq1, s_var1, f + 1)

            def step(f, m, b):
                if f is not None:
                    centre1(f)
                    dve.wait_ge(s_sd1, f + 1)
                    V.reciprocal(r1[:], sd1[:]).then_inc(s_r1, 1)
                    dve.wait_ge(s_r1, f + 1)
                    V.scalar_tensor_tensor(nm1[:], mean1[:], -0.5, r1[:], ALU.mult, ALU.mult).then_inc(s_nm1, 1)
                if m is not None:
                    for t in range(TG):
                        if t % TS == 0:
                            hold(s_y, SEQS * m + t // TS + 1)
                        V.bn_stats(st2[:, t, :], y[:, t // TS, t % TS * P:(t % TS + 1) * P]).then_inc(s_st2, 1)
                    dve.wait_ge(s_st2, TG * (m + 1))
                    moments(st2, mean2[:], dif2[:], m2_2[:], sq2[:], var2[:], s_half2, s_sq2, s_var2, m + 1)
                    dve.wait_ge(s_sd2, m + 1)
                    V.reciprocal(r2[:], sd2[:]).then_inc(s_r2, 1)
                    dve.wait_ge(s_r2, m + 1)
                    V.scalar_tensor_tensor(shift2[:, bass.ds(m * TG, TG)], mean2[:], -0.5, r2[:],
                                           ALU.mult, ALU.mult)
                if b is not None:
                    top2(b, m)
                elif m is not None:
                    for t in range(TG + 1):
                        residual(m, t)
                if m is not None:
                    dve.wait_ge(s_st3, TG * (m + 1))
                    moments(st3, mean3[:], dif3[:], m2_3[:], sq3[:], var3[:], s_half3, s_sq3, s_var3, m + 1)
                if f is not None:
                    dve.wait_ge(s_qkvp, SEQS * (f + 1))
                    V.tensor_copy(qk[:], qkv[:, :, 0:D]).then_inc(s_qk, 1)
                if m is not None:
                    dve.wait_ge(s_sd3, m + 1)
                    V.reciprocal(r3[:], sd3[:]).then_inc(s_r3, 1)
                if f is not None:
                    dve.wait_ge(s_qk, f + 1)
                    V.tensor_tensor(prod[:], qk[:], qkv[:, :, D:2 * D], ALU.mult).then_inc(s_prod, 1)
                if m is not None:
                    dve.wait_ge(s_r3, m + 1)
                    V.scalar_tensor_tensor(nm3[:], mean3[:], -0.5, r3[:], ALU.mult, ALU.mult).then_inc(s_nm3, 1)
                if f is not None:
                    V.tensor_tensor(vw[:], qkv[:, :, 2 * D:3 * D], every(fv, SEQS), ALU.mult).then_inc(s_vw, 1)
                    dve.wait_ge(s_prod, f + 1)
                    V.tensor_tensor(prodw[:], prod[:], every(fqk[:], SEQS), ALU.mult).then_inc(s_prodw, 1)
                    dve.wait_ge(s_prodw, f + 1)
                    V.tensor_reduce(red[:], prodw[:].rearrange("p s (h e) -> p (s h) e", e=HD), AX.X,
                                    ALU.add).then_inc(s_red, 1)
                if b is not None:
                    route(b, f)
                elif f is not None:
                    largest(f)
                    negated(f)
                    total(f)
                    inverted(f)
                    weighted(f)
                if f is not None:
                    dve.wait_ge(s_at, f + 1)
                    dve.wait_ge(s_vw, f + 1)
                    V.tensor_tensor(of[:].rearrange("p s (h e) -> p (s h) e", e=HD),
                                    vw[:].rearrange("p s (h e) -> p (s h) e", e=HD),
                                    wide(small[:, M:M + NH], HD), ALU.mult).then_inc(s_of, 1)

            def residual(m, t):
                if t < TG:
                    V.scalar_tensor_tensor(row(x, m * TG + t), y[:, t // TS, t % TS * P:(t % TS + 1) * P],
                                           r2[:, t:t + 1], row(x, m * TG + t), ALU.mult, ALU.add).then_inc(s_x1, 1)
                if t > 0:
                    hold(s_x1, m * TG + t)
                    V.bn_stats(st3[:, t - 1, :], row(x, m * TG + t - 1)).then_inc(s_st3, 1)

            def largest(f):
                dve.wait_ge(s_sc, f + 1)
                V.tensor_reduce(mx[:], small[0:NH, 0:M], AX.X, ALU.max).then_inc(s_mx, 1)

            def negated(f):
                dve.wait_ge(s_mx, f + 1)
                V.tensor_scalar(nmx[:], mx[:], 0.0, -1.0, ALU.max, ALU.mult).then_inc(s_nmx, 1)

            def total(f):
                dve.wait_ge(s_ex, 2 * (f + 1))
                V.scalar_tensor_tensor(tot[:], ex0[:], CUT, exs[:], ALU.mult, ALU.add).then_inc(s_tot, 1)

            def inverted(f):
                dve.wait_ge(s_tot, f + 1)
                V.reciprocal(rtot[:], tot[:]).then_inc(s_rtot, 1)

            def weighted(f):
                dve.wait_ge(s_rtot, f + 1)
                V.tensor_scalar(attn[:], every(ex[:], 2), rtot[:, 0:1], None, ALU.mult).then_inc(s_attn, 1)

            logits = route_[:, 0:TG * E].rearrange("p (t e) -> p t e", e=E)
            prefix = route_[:, 64:64 + TG * E].rearrange("p (e t) -> p e t", t=TG)
            totals = route_[:, 128:128 + TG * E]

            def top2(b, m):
                dve.wait_ge(s_lg, b + 1)
                n = [TOP * b, 0]

                def then(ins):
                    ins.then_inc(s_top, 1)
                    if m is not None and n[1] <= TG:
                        residual(m, n[1])
                    n[0], n[1] = n[0] + 1, n[1] + 1
                    dve.wait_ge(s_top, n[0])

                then(V.tensor_reduce(m1[:], logits, AX.X, ALU.max))
                then(V.tensor_tensor(eq[:], logits, wide(m1[:], E), ALU.is_equal))
                then(V.tensor_tensor(eqd[:], eq[:], every(e_down, TG), ALU.mult))
                then(V.tensor_reduce(i1[:], eqd[:], AX.X, ALU.max))
                then(V.tensor_tensor(oh1[:], every(e_down, TG), wide(i1[:], E), ALU.is_equal))
                then(V.scalar_tensor_tensor(rest[:], oh1[:], -BIG, logits, ALU.mult, ALU.add))
                then(V.tensor_reduce(m2[:], rest[:], AX.X, ALU.max))
                then(V.tensor_tensor(eq[:], rest[:], wide(m2[:], E), ALU.is_equal))
                then(V.tensor_tensor(eqd[:], eq[:], every(e_down, TG), ALU.mult))
                then(V.tensor_reduce(i2[:], eqd[:], AX.X, ALU.max))
                then(V.tensor_tensor(oh2[:], every(e_down, TG), wide(i2[:], E), ALU.is_equal))
                V.tensor_tensor(gap[:, bass.ds(b * TG, TG)], m1[:], m2[:], ALU.subtract).then_inc(s_gap, 1)
                V.tensor_tensor(cnt[:].rearrange("p e t -> p t e"), oh1[:], oh2[:], ALU.add).then_inc(s_cnt, 1)

            def route(b, f):
                n = RT * b

                def then(ins, between=None):
                    nonlocal n
                    ins.then_inc(s_rt, 1)
                    if between is not None and f is not None:
                        between(f)
                    n = n + 1
                    dve.wait_ge(s_rt, n)

                dve.wait_ge(s_pfx, b + 1)
                then(V.tensor_tensor_scan(inc[:].rearrange("p e t -> p (e t)"), t_keep, totals, 0.0, ALU.mult, ALU.add))
                then(V.tensor_scalar(up[:], inc[:, :, TG - 1], float(P - 1), None, ALU.add))
                then(V.tensor_scalar(tiles[:], up[:], 7, None, ALU.arith_shift_right))
                then(V.tensor_tensor_scan(cum[:], ones[:, 0:E], tiles[:], 0.0, ALU.mult, ALU.add))
                then(V.tensor_tensor(base[:], cum[:], tiles[:], ALU.subtract), largest)
                then(V.tensor_tensor(pos[:], inc[:], totals.rearrange("p (e t) -> p e t", t=TG), ALU.subtract), negated)
                then(V.tensor_tensor(pos2[:], pos[:], prefix, ALU.add))
                then(V.scalar_tensor_tensor(slot[:], wide(base[:], TG), float(P), pos2[:], ALU.mult, ALU.add))
                by_tile = slot[:].rearrange("p e t -> p t e")
                then(V.tensor_tensor(pick1[:], oh1[:], by_tile, ALU.mult), total)
                V.tensor_reduce(slots[:, bass.ds(b, 1), 0, :].rearrange("p a t -> p (a t)"), pick1[:], AX.X,
                                ALU.add).then_inc(s_slots, 1)
                then(V.tensor_tensor(pick2[:], oh2[:], by_tile, ALU.mult), inverted)
                V.tensor_reduce(slots[:, bass.ds(b, 1), 1, :].rearrange("p a t -> p (a t)"), pick2[:], AX.X,
                                ALU.add).then_inc(s_slots, 1)
                then(V.tensor_tensor(before[:].rearrange("p (j e) -> p j e", e=7), every(cum[0:1, 0:7], TPG * ROW),
                                     j_row[0:1].rearrange("p (j e) -> p j e", e=7), ALU.is_le), weighted)
                V.tensor_reduce(expert[:], before[:].rearrange("p (j e) -> p j e", e=7), AX.X, ALU.add).then_inc(s_cols, 1)
                dve.wait_ge(s_cols, 2 * b + 1)
                V.tensor_scalar(columns[:, bass.ds(b * TPG * ROW, TPG * ROW)], expert[:], float(2 * F), None,
                                ALU.mult).then_inc(s_cols, 1)

            dve.wait_ge(s_front, 16)
            V.tensor_tensor(fold[:, :], ident[:, 0:M], ident[:, M:2 * M], ALU.add).then_inc(s_const, 1)
            V.tensor_tensor(fqk[:], fq, fk, ALU.mult).then_inc(s_fqk, 1)
            dve.wait_ge(s_bias, 16)
            V.tensor_scalar(bqkv[:], bias[:, BIAS["bqkv"]], float(S), None, ALU.mult).then_inc(s_const, 1)
            dve.wait_ge(s_fqk, 1)
            step(0, None, None)
            dve.wait_ge(s_back, 16)
            V.tensor_copy(tri[:], tri_f).then_inc(s_const, 1)
            step(1, 0, None)
            step(2, 1, 0)
            with dve.Fori(0, NG - 3) as i:
                step(i + 3, i + 2, i + 1)
            step(None, NG - 1, NG - 2)
            step(None, None, NG - 1)
            dve.wait_ge(s_e2, 1)
            V.tensor_scalar(e2p[:], e2[:], 1.0, None, ALU.add).then_inc(s_wt, 1)
            dve.wait_ge(s_wt, 1)
            V.reciprocal(wt1[:], e2p[:]).then_inc(s_wt, 1)
            dve.wait_ge(s_wt, 2)
            V.tensor_tensor(wt2[:], wt1[:], e2[:], ALU.mult).then_inc(s_wt, 1)
            dve.wait_ge(s_wt, 3)

            def low(j, k):
                dve.wait_ge(s_xh, j + 1)
                V.tensor_tensor(xl[:, k % 2, :], pb[k % 2][:, 0:P], xh[:, k % 2, :].bitcast(F32),
                                ALU.subtract).then_inc(s_xl, 1)

            def hidden(j, k):
                dve.wait_ge(s_silu, j + 1)
                V.tensor_tensor(hid[:, k % 2, :], pb[2 + k % 2][:, F:2 * F], gate[:, k % 2, :],
                                ALU.mult).then_inc(s_h, 1)

            def tile_step(j, k, last=False):
                if not (last and k + AHEAD + 1 >= STEP):
                    low(j + AHEAD + 1, k + AHEAD + 1)
                if not (last and k + AHEAD >= STEP):
                    hidden(j + AHEAD, k + AHEAD)

            def first_row(k, odd):
                dve.wait_ge(s_gat[odd], (k >> 1) * 32 + 32)
                V.tensor_scalar(row(za, wrap(k)), row(ya, wrap(k)), wt1[:, bass.ds(k, 1)], None,
                                ALU.mult).then_inc(s_za, 1)

            def second_row(k):
                dve.wait_ge(s_za, k + 1)
                V.scalar_tensor_tensor(row(za, wrap(k)), row(yb, wrap(k)), wt2[:, bass.ds(k, 1)], row(za, wrap(k)),
                                       ALU.mult, ALU.add).then_inc(s_z, 1)

            def sum_moments(k):
                hold(s_z, k + 1)
                V.bn_stats(row(stz, k), row(za, wrap(k))).then_inc(s_stz, 1)

            def variances(g):
                part = slice(g * TG, (g + 1) * TG)
                dve.wait_ge(s_stz, TG * (g + 1))
                moments(stz[:, part, :], meanz[:, part], difz[:, part], m2_z[:, part], sqz[:, part],
                        varz[:, part], s_halfz, s_sqz, s_sumz, g + 1)
                dve.wait_ge(s_sumz, g + 1)
                V.tensor_scalar(var[:, part], varz[:, part], 1.0 / D, EPS, ALU.mult, ALU.add).then_inc(s_var, 1)

            def shifts(g):
                part = slice(g * TG, (g + 1) * TG)
                dve.wait_ge(s_rz, g + 1)
                V.scalar_tensor_tensor(cz[:, part], meanz[:, part], -0.5, rz[:, part], ALU.mult,
                                       ALU.mult).then_inc(s_cz, 1)
                dve.wait_ge(s_cz, 2 * g + 1)
                V.tensor_tensor(shift[:, part], cz[:, part], shift2[:, part], ALU.add).then_inc(s_cz, 1)
                dve.wait_ge(s_cz, 2 * g + 2)

            def scaled(k):
                V.scalar_tensor_tensor(row(zn, k), row(za, wrap(k)), rz[:, bass.ds(k, 1)], row(x, k), ALU.mult,
                                       ALU.add).then_inc(s_zn, 1)

            def shifted(k):
                dve.wait_ge(s_zn, k + 1)
                V.tensor_scalar(row(x, k), row(zn, k), shift[:, bass.ds(k, 1)], None, ALU.add).then_inc(s_out, 1)

            def sums_of(tiles_):
                n = len(tiles_)
                for i in range(n + 2):
                    if i < n:
                        first_row(tiles_[i], tiles_[i] % 2)
                    if 0 <= i - 1 < n:
                        second_row(tiles_[i - 1])
                    if 0 <= i - 2 < n:
                        sum_moments(tiles_[i - 2])

            def finals_of(tiles_):
                n = len(tiles_)
                for i in range(n + 1):
                    if i < n:
                        scaled(tiles_[i])
                    if i:
                        shifted(tiles_[i - 1])

            def wrap(k):
                return k % (2 * TG) if isinstance(k, int) else k & (2 * TG - 1)

            def turn_of(turn, sums, finals, last=False):
                for k in range(STEP):
                    tile_step(turn * STEP + k, k, last)
                    summed, normed = (turn - ZLAG) * ZT + k // 3, (turn - NLAG) * ZT + k // 3
                    if k % 3 == 0:
                        if sums:
                            first_row(summed, k // 3)
                        if finals:
                            scaled(normed)
                    elif k % 3 == 1:
                        if sums:
                            second_row(summed)
                        if finals:
                            shifted(normed)
                    elif sums:
                        sum_moments(summed)

            low(0, 0)
            low(1, 1)
            hidden(0, 0)
            low(2, 2)
            hidden(1, 1)
            low(3, 3)
            hidden(2, 2)
            turn_of(0, False, False)
            with dve.Fori(1, ZLAG) as turn:
                turn_of(turn, False, False)
            with dve.Fori(ZLAG, NLAG) as turn:
                turn_of(turn, True, False)
            variances(0)
            for g in range(1, NG):
                first = NLAG + (g - 1) * TPG
                if first >= TURNS:
                    break
                end = min(first + TPG, TURNS - 1)
                turn_of(first, True, False)
                shifts(g - 1)
                finals_of(range((g - 1) * TG, (g - 1) * TG + ZT))
                with dve.Fori(first + 1, end) as turn:
                    turn_of(turn, True, True)
                if end < first + TPG:
                    turn_of(TURNS - 1, True, True, last=True)
                else:
                    variances(g)
            summed = (TURNS - ZLAG) * ZT
            normed = (TURNS - NLAG) * ZT
            for g in range(normed // TG, NG):
                if summed < (g + 1) * TG:
                    sums_of(range(summed, (g + 1) * TG))
                    variances(g)
                    summed = (g + 1) * TG
                if normed == g * TG:
                    shifts(g)
                finals_of(range(normed, (g + 1) * TG))
                normed = (g + 1) * TG

        @block.tensor
        def _(pe):
            T = nc.tensor
            pe.wait_ge(s_front, 16)
            pe.wait_ge(s_const, 4)

            def step(f, m, b):
                if m is not None:
                    pe.wait_ge(s_of, m + 1)
                    for q in range(SEQS):
                        ins = T.transpose(of_t[:, q * P:(q + 1) * P], of[:, q, :], ident)
                    ins.then_inc(s_oftp, 1)
                    for q in range(SEQS):
                        T.matmul(z_[:, q * P:(q + 1) * P], ident[0:1, :], bout, start=True, stop=False)
                        if q == 0:
                            pe.wait_ge(s_oft, m + 1)
                        ins = T.matmul(z_[:, q * P:(q + 1) * P], oft[:, q, :], wout,
                                       start=False, stop=True)
                    ins.then_inc(s_zp, 1)
                for q in range(SEQS):
                    if b is not None:
                        pe.wait_ge(s_xn2, TG * b + TS * (q + 1))
                        for t in range(TS):
                            ins = T.transpose(qkv[:, q, t * P:(t + 1) * P], xn2[:, q * TS + t, :], ident)
                        ins.then_inc(s_xn2p, 1)
                    if m is not None:
                        if q == 0:
                            pe.wait_ge(s_zs, m + 1)
                        for t in range(TS):
                            ins = T.matmul(y[:, q, t * P:(t + 1) * P], ginv[:, t * P:(t + 1) * P], zs[:, q, :],
                                           start=True, stop=True)
                        ins.then_inc(s_y, 1)
                if b is not None:
                    if f is None:
                        pe.wait_ge(s_slots, 2 * b)
                    for q in range(SEQS):
                        pe.wait_ge(s_xn2t, SEQS * b + q + 1)
                        for t in range(TS):
                            n = q * TS + t
                            ins = T.matmul(route_[:, n * E:(n + 1) * E], xn2t[:, q, t * P:(t + 1) * P], rw,
                                           start=True, stop=True)
                    ins.then_inc(s_lg, 1)
                if f is not None:
                    for q in range(SEQS):
                        pe.wait_ge(s_xn, TG * f + TS * (q + 1))
                        for t in range(TS):
                            ins = T.matmul(dft_[:, q * P:(q + 1) * P], xn[:, q * TS + t, :], ftab[:, t, :],
                                           start=(t == 0), stop=(t == TS - 1))
                    ins.then_inc(s_dft, 1)
                    for q in range(SEQS):
                        T.matmul(qkv[:, q, 0:3 * D], ident[0:1, :], bqkv[:], start=True, stop=False)
                    pe.wait_ge(s_xft, f + 1)
                    for q in range(SEQS):
                        T.matmul(qkv[:, q, 0:3 * D], xft[:, q, :], wqkv, start=False, stop=True).then_inc(s_qkvp, 1)
                    pe.wait_ge(s_red, f + 1)
                    T.matmul(small[0:NH, 0:M], red[:], fold[:], start=True, stop=True).then_inc(s_sc, 1)
                if b is not None:
                    pe.wait_ge(s_cnt, b + 1)
                    flat = cnt[:].rearrange("p e t -> p (e t)")
                    T.matmul(route_[:, 64:128], tri[:], flat, start=True, stop=True)
                    T.matmul(route_[:, 128:192], ones[:], flat, start=True, stop=True).then_inc(s_pfx, 1)
                if f is not None:
                    pe.wait_ge(s_attn, f + 1)
                    T.matmul(small[:, M:M + NH], attn[:].rearrange("h a m -> h (a m)"), ident[0:NH, 0:NH],
                             start=True, stop=True).then_inc(s_at, 1)

            step(0, None, None)
            pe.wait_ge(s_back, 16)
            pe.wait_ge(s_const, 5)
            step(1, 0, None)
            step(2, 1, 0)
            with pe.Fori(0, NG - 3) as i:
                step(i + 3, i + 2, i + 1)
            step(None, NG - 1, NG - 2)
            step(None, None, NG - 1)
            pe.wait_ge(s_cols, 2 * NG)
            pe.wait_ge(s_slots, 2 * NG)
            pe.wait_ge(s_w13, 2)
            pe.wait_ge(s_we, 16 * N_EXP)

            def turned(j, k, turn):
                if k % STEP == 0:
                    pe.wait_ge(s_xeA, 16 * (turn + 1))
                if k % STEP == HALF:
                    pe.wait_ge(s_xeB, 16 * (turn + 1))
                T.transpose(pb[k % 2][:, 0:P], xe[:, k % STEP, :], ident).then_inc(s_xt, 1)

            cols = [pe.alloc_register(f"columns_{k}") for k in range(STEP + AHEAD)]

            def experts_of(turn, n, first=0):
                pe.load(cols[first:first + n], columns[0:1, bass.ds(turn * ROW, n)])
                return [pe.snap(r, min_val=0, max_val=(E - 1) * 2 * F) for r in cols[first:first + n]]

            def gate_up(j, k, col):
                pe.wait_ge(s_xl, j + 1)
                out_, c = pb[2 + k % 2][:], k % 2
                hi, lo = w13h[:, bass.ds(col, 2 * F)], w13l[:, bass.ds(col, 2 * F)]
                T.matmul(out_, xh[:, c, :], hi, start=True, stop=False)
                T.matmul(out_, xh[:, c, :], lo, start=False, stop=False)
                T.matmul(out_, xl[:, c, :], hi, start=False, stop=True).then_inc(s_gu, 1)

            def hidden_turned(j, k):
                pe.wait_ge(s_h, j + 1)
                for c in range(FC):
                    ins = T.transpose(pb[4 + k % 2][:, c * P:(c + 1) * P], hid[:, k % 2, c * P:(c + 1) * P], ident)
                ins.then_inc(s_ht, 1)

            def down(j, k, col):
                pe.wait_ge(s_hc, j + 1)
                for c in range(FC):
                    ins = T.matmul(pb[6 + k % 2][:, 0:D], hidt[:, k % 2, c * P:(c + 1) * P],
                                   w2[:, bass.ds(col + c * D, D)], start=(c == 0), stop=(c == FC - 1))
                ins.then_inc(s_dn, 1)

            def transposes(j, k, turn, last=False):
                if not (last and k + 1 >= STEP):
                    hidden_turned(j + 1, k + 1)
                if not (last and k + AHEAD + 1 >= STEP):
                    turned(j + AHEAD + 1, k + AHEAD + 1, turn + (k + AHEAD + 1) // STEP)

            def products(j, k, exp, last=False):
                if not (last and k + AHEAD >= STEP):
                    gate_up(j + AHEAD, k + AHEAD, exp[k + AHEAD])
                down(j, k, exp[k])

            exp = experts_of(0, STEP)
            turned(0, 0, 0)
            turned(1, 1, 0)
            gate_up(0, 0, exp[0])
            turned(2, 2, 0)
            gate_up(1, 1, exp[1])
            hidden_turned(0, 0)
            turned(3, 3, 0)
            gate_up(2, 2, exp[2])
            exp += experts_of(1, AHEAD, STEP)
            for k in range(STEP):
                transposes(k, k, 0)
                products(k, k, exp)
            with pe.Fori(1, TURNS - 1) as turn:
                for k in range(STEP):
                    transposes(turn * STEP + k, k, turn)
                    if k == 0:
                        exp = experts_of(turn, STEP) + experts_of(turn + 1, AHEAD, STEP)
                    products(turn * STEP + k, k, exp)
            for k in range(STEP):
                j = (TURNS - 1) * STEP + k
                transposes(j, k, TURNS - 1, last=True)
                if k == 0:
                    exp = experts_of(TURNS - 1, STEP)
                products(j, k, exp, last=True)


def kernel(L0_attn_query, L0_attn_w_qkv, L0_attn_b_qkv, L0_attn_w_out, L0_attn_b_out, L0_attn_freq_q,
           L0_attn_freq_k, L0_attn_freq_v, L0_ffn_router_w, L0_ffn_w1, L0_ffn_w3, L0_ffn_w2):
    import concourse.bacc as bacc
    from concourse.bass_utils import run_bass_kernel_spmd

    f32 = np.float32

    def both_halves(w):
        w = np.transpose(np.asarray(w), (1, 0, 2)).reshape(M, D)
        return np.concatenate([w, w], axis=0)

    angle = 2 * np.pi * (np.outer(np.arange(S), np.arange(M)) % S) / S
    ftab = np.concatenate([np.cos(angle), np.sin(angle)], axis=1).astype(f32)
    w_qkv, w_out = np.asarray(L0_attn_w_qkv), np.asarray(L0_attn_w_out)
    front = {"ftab": ftab.reshape(TS, P, P).transpose(1, 0, 2).reshape(P, TS * P), "wqkv": w_qkv.T,
             "ident": np.eye(P, dtype=f32), "fq": both_halves(L0_attn_freq_q), "fk": both_halves(L0_attn_freq_k),
             "fv": both_halves(L0_attn_freq_v)}
    tile = np.repeat((np.arange(TPG)[:, None] * STEP + np.arange(ROW)).ravel(), E - 1)
    back = {"ginv": ftab.T, "wout": w_out.T, "rw": np.asarray(L0_ffn_router_w),
            "tri": np.triu(np.ones((P, P), f32), 1), "down": np.tile(8 - np.arange(E, dtype=f32), (P, 1)),
            "keep": np.tile((np.arange(TG) > 0).astype(f32), (P, E)), "tile": np.tile(tile.astype(f32), (P, 1))}
    bias = np.concatenate([np.asarray(L0_attn_b_qkv), np.asarray(L0_attn_b_out)])[None]
    w1, w3, w2 = (np.asarray(w) for w in (L0_ffn_w1, L0_ffn_w3, L0_ffn_w2))
    arrays = {
        "query": np.asarray(L0_attn_query).reshape(B * S, D),
        "front": np.concatenate([front[name] for name in FRONT], axis=1),
        "back": np.concatenate([back[name] for name in BACK], axis=1),
        "bias": bias,
        "w13": np.concatenate([w1, w3], axis=2).transpose(1, 0, 2).reshape(D, E * 2 * F),
        "w2": w2.reshape(E, FC, P, D).transpose(2, 0, 1, 3).reshape(P, E * FC * D),
    }
    nc = bacc.Bacc("TRN2", target_bir_lowering=False, num_devices=1)
    ins, args = {}, []
    for name, a in arrays.items():
        ins[f"in_{name}"] = np.ascontiguousarray(a)
        args.append(nc.dram_tensor(f"in_{name}", a.shape, mybir.dt.from_np(a.dtype), kind="ExternalInput").ap())
    out = nc.dram_tensor("out_x", (B * S, D), F32, kind="ExternalOutput").ap()
    build(nc, *args, out)
    r = run_bass_kernel_spmd(nc, [ins], core_ids=[0])
    return r.results[0]["out_x"].reshape(B, S, D)
```

```python
from contextlib import ExitStack

import numpy as np

import concourse.bass as bass
from concourse import mybir

ALU = mybir.AluOpType
ACT = mybir.ActivationFunctionType
AX = mybir.AxisListType
F32 = mybir.dt.float32
F32R = mybir.dt.float32r
BF16 = mybir.dt.bfloat16
I32 = mybir.dt.int32

P = 128
B, S, D = 8, 512, 128
H, M, HD = 16, 64, 8
E, F = 8, 256
FC = F // P
EPS = 1e-5
CUT = float(S - M)

TS = S // P
SEQS = 2
NG = B // SEQS
TG = TS * SEQS
NT = NG * TG
STEP = 8
HALF = STEP // 2
AHEAD = 3
BATCHES = ((0, 1), (1, 3), (3, 4))
NB = len(BATCHES)
BT = [(end - first) * TG for first, end in BATCHES]
BTURNS = [-(-(2 * n + E - 1) // STEP) for n in BT]
FIRST = [sum(BTURNS[:r]) for r in range(NB)]
TURNS = sum(BTURNS)
MOST = max(BT)
ET = max(BTURNS) * STEP
RING = 2 * TG
ZT = 4
ZTURNS = BTURNS[0] + 1, BTURNS[0] + 1 + BT[0] // ZT
NTURNS = ZTURNS[1] + 1, ZTURNS[1] + 1 + BT[0] // ZT
LATE = FIRST[2] + 1
PARTS = ((TG, 3 * TG), (3 * TG, NT - 2), (NT - 2, NT))
OUTS = tuple((k, k + ZT) for k in range(0, NT - ZT, ZT)) + ((NT - ZT, NT - 2), (NT - 2, NT))
WAIT_START, WAIT_RED, WAIT_ATTENTION, WAIT_OF, WAIT_Z, WAIT_COUNTS = 100, 16, 36, 20, 16, 34
WAIT_LAST, WAIT_LOW = 16, 10
BIG = 3.0e38

assert STEP % 2 == 0 and NTURNS[1] <= LATE <= TURNS - 1


def at_least(eng, sem, n):
    if isinstance(n, int) and n <= 0:
        return
    eng.wait_ge(sem, n)


def parts(widths):
    at, n = {}, 0
    for name, w in widths:
        at[name] = slice(n, n + w)
        n += w
    return at, n


FRONT, N_FRONT = parts([("ftab", TS * P), ("wqkv", 3 * D), ("ident", P), ("fq", D), ("fk", D), ("fv", D)])
BACK, N_BACK = parts([("ginv", S), ("wout", D), ("rw", E), ("tri", P), ("down", E), ("keep_small", E * TG), ("keep", E * MOST),
                      ("tile", ET * (E - 1))])
BIAS, N_BIAS = parts([("bqkv", 3 * D), ("bout", D)])


def build(nc, x_in, front_in, back_in, bias_in, w13_in, w2_in, out):
    with ExitStack() as ctx:
        ctx.enter_context(nc.allow_low_precision(reason="sums of small whole numbers, kept as integers"))

        def sb(name, shape, dt=F32):
            return ctx.enter_context(nc.sbuf_tensor(name, shape, dt))

        def bank(name):
            return ctx.enter_context(nc.psum_tensor(name, [P, 512], F32))

        def sem(name):
            return ctx.enter_context(nc.semaphore(name))

        front = sb("front", [P, N_FRONT])
        ftab = front[:, FRONT["ftab"]].rearrange("p (t f) -> p t f", t=TS)
        wqkv = front[:, FRONT["wqkv"]]
        ident = front[:, FRONT["ident"]]
        fq, fk, fv = front[:, FRONT["fq"]], front[:, FRONT["fk"]], front[:, FRONT["fv"]]
        back = sb("back", [P, N_BACK])
        ginv = back[:, BACK["ginv"]]
        wout = back[:, BACK["wout"]]
        rw = back[:, BACK["rw"]]
        tri_f = back[:, BACK["tri"]]
        e_down = back[:, BACK["down"]]
        t_keep = {TG: back[:, BACK["keep_small"]], MOST: back[:, BACK["keep"]]}
        j_row = back[:, BACK["tile"]]
        bias = sb("bias", [1, N_BIAS])
        bout = bias[:, BIAS["bout"]]
        bqkv = sb("bqkv", [1, 3 * D])
        tri = sb("tri", [P, P], BF16)
        ones = sb("ones", [P, P], BF16)
        fold = sb("fold", [P, M])
        eps = sb("eps", [P, 1])
        fqk = sb("fqk", [P, D])
        w13 = sb("w13", [P, E * 2 * F])
        w13h = sb("w13h", [P, E * 2 * F], F32R)
        w13l = sb("w13l", [P, E * 2 * F], F32R)
        w2 = sb("w2", [P, E * 2 * F])
        zero = sb("zero", [P, STEP * P])

        x = sb("x", [P, NT, D])
        shift2 = sb("shift2", [P, NT])

        st1 = sb("st1", [P, NT, 6])
        mean1 = sb("mean1", [P, NT])
        dif1 = sb("dif1", [P, NT])
        m2_1 = sb("m2_1", [P, NT])
        sq1 = sb("sq1", [P, NT])
        var1 = sb("var1", [P, NT])
        sd1 = sb("sd1", [P, NT])
        r1 = sb("r1", [P, NT])
        nm1 = sb("nm1", [P, NT])
        xn = sb("xn", [P, TG, D])
        xft = sb("xft", [P, SEQS, P])
        qw = sb("qw", [P, SEQS, D])
        prod = sb("prod", [P, SEQS, D])
        vw = sb("vw", [P, SEQS, D])
        red = sb("red", [P, SEQS * H])
        NH = SEQS * H
        mx = sb("mx", [NH, 1])
        nmx = sb("nmx", [NH, 1])
        ex = sb("ex", [NH, M])
        exs = sb("exs", [NH, 1])
        ex0 = sb("ex0", [NH, 1])
        tot = sb("tot", [NH, 1])
        rtot = sb("rtot", [NH, 1])
        attn = sb("attn", [NH, 2, M])
        of = sb("of", [P, SEQS, D])
        oft = sb("oft", [P, SEQS, P])
        zs = sb("zs", [P, SEQS, D])

        st2 = sb("st2", [P, TG, 6])
        mean2 = sb("mean2", [P, TG])
        dif2 = sb("dif2", [P, TG])
        m2_2 = sb("m2_2", [P, TG])
        sq2 = sb("sq2", [P, TG])
        var2 = sb("var2", [P, TG])
        sd2 = sb("sd2", [P, TG])
        r2 = sb("r2", [P, TG])
        st3 = sb("st3", [P, TG, 6])
        mean3 = sb("mean3", [P, TG])
        dif3 = sb("dif3", [P, TG])
        m2_3 = sb("m2_3", [P, TG])
        sq3 = sb("sq3", [P, TG])
        var3 = sb("var3", [P, TG])
        sd3 = sb("sd3", [P, TG])
        r3 = sb("r3", [P, TG])
        nm3 = sb("nm3", [P, TG])
        xn2 = sb("xn2", [P, NT, D])
        var3e = sb("var3e", [P, TG])
        xn2t = sb("xn2t", [P, SEQS, S])

        m1 = sb("m1", [P, TG])
        m2 = sb("m2", [P, TG])
        i1 = sb("i1", [P, TG])
        i2 = sb("i2", [P, TG])
        eq = sb("eq", [P, TG, E])
        eqd = sb("eqd", [P, TG, E])
        oh1 = sb("oh1", [P, MOST, E])
        oh2 = sb("oh2", [P, MOST, E])
        rest = sb("rest", [P, TG, E])
        last_logits = sb("last_logits", [P, TG * E])
        last_sums = sb("last_sums", [P, 2, E * TG])
        gap = sb("gap", [P, NT])
        e2 = sb("e2", [P, NT])
        e2p = sb("e2p", [P, NT])
        wt1 = sb("wt1", [P, NT])
        wt2 = sb("wt2", [P, NT])
        cnt = sb("cnt", [P, E * MOST], BF16)
        inc = sb("inc", [P, E * MOST])
        pos = sb("pos", [P, E * MOST])
        pos2 = sb("pos2", [P, E * MOST])
        up = sb("up", [P, E], I32)
        tiles = sb("tiles", [P, E], I32)
        cum = sb("cum", [P, E])
        base = sb("base", [P, E])
        slot = sb("slot", [P, E * MOST])
        pick1 = sb("pick1", [P, MOST, E])
        pick2 = sb("pick2", [P, MOST, E])
        slots = sb("slots", [P, 2, NT], I32)
        before = sb("before", [1, ET * 7])
        expert = sb("expert", [1, ET])
        columns = sb("columns", [1, TURNS * STEP], I32)

        xe = sb("xe", [P, STEP, D])
        xh = sb("xh", [P, 2, P], F32R)
        xl = sb("xl", [P, 2, P], F32R)
        gate = sb("gate", [P, 2, F])
        hid = sb("hid", [P, 2, F])
        hidt = sb("hidt", [P, 2, F])
        ye = sb("ye", [P, STEP, D])

        ya = sb("ya", [P, RING, D])
        yb = sb("yb", [P, RING, D])
        za = sb("za", [P, NT, D])
        stz = sb("stz", [P, NT, 6])
        meanz = sb("meanz", [P, NT])
        difz = sb("difz", [P, NT])
        m2_z = sb("m2_z", [P, NT])
        sqz = sb("sqz", [P, NT])
        varz = sb("varz", [P, NT])
        var = sb("var", [P, BT[0]])
        rz = sb("rz", [P, NT])
        sdz = sb("sdz", [P, NT])
        cz = sb("cz", [P, NT])
        shift = sb("shift", [P, NT])
        half = sb("half", [P, TG])
        zn = xn2

        pair = [ctx.enter_context(nc.psum_tensor(f"pair{i}", [P, 2, 512], F32)) for i in range(4)]
        pb = [pair[i // 2][:, i % 2, :] for i in range(8)]
        dft_, small, z_, of_t, route_ = pb[0][:, 0:SEQS * P], pb[1], pb[1][:, P:(SEQS + 1) * P], pb[4], pb[5]
        turned3 = pb[4], pb[0]
        qkv, y = pair[1], pair[3]

        xg, yg = ([nc.dram_tensor(f"{name}{r}", [BTURNS[r] * STEP * P, D], F32, kind="Internal").ap()
                   for r in range(NB)] for name in ("xg", "yg"))

        s_held = sem("waits_passed")
        s_x = sem("x_loaded")
        s_front = sem("front_weights_loaded")
        s_back = sem("back_weights_loaded")
        s_bias = sem("biases_loaded")
        s_we = sem("expert_weights_loaded")
        s_const = sem("constants_ready")
        s_halves = sem("exponents_ready")
        s_fqk = sem("filters_multiplied")
        s_w13 = sem("w13_split")
        s_zero = sem("zero_tile_ready")
        s_xgz = sem("slots_zeroed")
        s_st1 = sem("stats1")
        s_half1 = sem("halves_joined1")
        s_sq1 = sem("difference_squared1")
        s_var1 = sem("variance1")
        s_sd1 = sem("deviation1")
        s_r1 = sem("reciprocal1")
        s_nm1 = sem("shift1_ready")
        s_xn = sem("xn_ready")
        s_dft = sem("dft_done")
        s_xft = sem("xft_copied")
        s_qkvp = sem("qkv_done")
        s_qw = sem("q_filtered")
        s_prod = sem("qk_product")
        s_vw = sem("v_filtered")
        s_red = sem("qk_summed")
        s_sc = sem("scores_done")
        s_mx = sem("max_taken")
        s_nmx = sem("max_negated")
        s_ex = sem("exp_done")
        s_tot = sem("sum_done")
        s_rtot = sem("sum_inverted")
        s_attn = sem("attention_ready")
        s_at = sem("attention_turned")
        s_of = sem("of_ready")
        s_oftp = sem("of_turned")
        s_oft = sem("oft_copied")
        s_zp = sem("z_done")
        s_zs = sem("z_biased")
        s_y = sem("y_done")
        s_st2 = sem("stats2")
        s_half2 = sem("halves_joined2")
        s_sq2 = sem("difference_squared2")
        s_var2 = sem("variance2")
        s_sd2 = sem("deviation2")
        s_r2 = sem("reciprocal2")
        s_x1 = sem("x1_ready")
        s_st3 = sem("stats3")
        s_half3 = sem("halves_joined3")
        s_sq3 = sem("difference_squared3")
        s_var3 = sem("variance3")
        s_sd3 = sem("deviation3")
        s_r3 = sem("reciprocal3")
        s_nm3 = sem("shift3_ready")
        s_xn2 = sem("xn2_ready")
        s_xn2v = sem("xn2_ready_by_vector")
        s_var3e = sem("variance3_last")
        s_xn2p = sem("xn2_turned")
        s_xn2t = sem("xn2t_copied")
        s_lg = sem("logits_done")
        s_top = sem("top2_steps")
        s_cnt = sem("counts_ready")
        s_last = sem("last_batch_copied")
        s_pfx = sem("prefix_done")
        s_rt = sem("route_steps")
        s_slots = sem("slots_ready")
        s_cols = sem("columns_ready")
        s_scat = [sem(f"rows_scattered_{r}") for r in range(NB)]
        s_gap = sem("gaps_ready")
        s_e2 = sem("gap_exp")
        s_wt = sem("weights_of_pairs")
        s_xeA = sem("rows_loaded_a")
        s_xeB = sem("rows_loaded_b")
        s_xt = sem("tile_turned")
        s_xh = sem("tile_high")
        s_xl = sem("tile_low")
        s_gu = sem("gate_up_done")
        s_silu = sem("silu_done")
        s_h = sem("hidden_ready")
        s_ht = sem("hidden_turned")
        s_hc = sem("hidden_copied")
        s_dn = sem("down_done")
        s_ye = sem("tile_out")
        s_stA = sem("tiles_stored_a")
        s_stB = sem("tiles_stored_b")
        s_gat = [sem(f"pair_gathered_{i}") for i in range(ZT)]
        s_za = sem("first_weighted")
        s_z = sem("sum_ready")
        s_stz = sem("stats_z")
        s_halfz = sem("halves_joined_z")
        s_sqz = sem("difference_squared_z")
        s_sumz = sem("variance_summed_z")
        s_var = sem("variance_z")
        s_rz = sem("rsqrt_z")
        s_rz2 = sem("deviation_z_inverted")
        s_sdz = sem("deviation_z")
        s_cz = sem("shift_z")
        s_zn = sem("z_scaled")
        s_out = sem("out_ready")
        s_stored = sem("out_stored")

        x_dram = x_in.rearrange("(g t p) d -> g p t d", p=P, t=TG)
        out_dram = out.rearrange("(t p) d -> p t d", p=P)
        N_EXP = 2
        TOP, RT = 11, 11
        NORMED = 6
        LEAD = 4
        EARLY, PREFIX, ROUTED = 3, 9, 11

        block = ctx.enter_context(nc.Block())

        @block.sync
        def _(sp):
            for g in range(NG):
                at_least(sp, s_x, 16 * g)
                sp.dma_start(x[:, g * TG:(g + 1) * TG, :], x_dram[g]).then_inc(s_x, 16)
            sp.dma_start(w13[:], w13_in).then_inc(s_we, 16)
            sp.dma_start(w2[:].rearrange("p (e n) -> p e n", n=2 * F)[:, :, 0:FC * D],
                         w2_in.rearrange("p (e n) -> p e n", n=FC * D)).then_inc(s_we, 16)
            sp.wait_ge(s_zero, 1)
            for r in range(NB):
                for turn in range(BTURNS[r]):
                    part = xg[r][turn * STEP * P:(turn + 1) * STEP * P, :]
                    sp.dma_start(part.rearrange("(p j) d -> p (j d)", p=P), zero[:]).then_inc(s_xgz, 16)

            def batch_of(turn):
                return max(r for r in range(NB) if FIRST[r] <= turn)

            def tiles_of(dram, turn, half):
                r = batch_of(turn)
                at = ((turn - FIRST[r]) * STEP + half * HALF) * P
                return dram[r][at:at + HALF * P, :].rearrange("(j p) d -> p j d", p=P)

            def load(turn, half):
                if turn in FIRST:
                    r = batch_of(turn)
                    sp.wait_ge(s_scat[r], 16 * 2 * BT[r])
                at_least(sp, s_xt, STEP * (turn - 1) + HALF * (half + 1))
                sp.dma_start(xe[:, half * HALF:(half + 1) * HALF, :], tiles_of(xg, turn, half)).then_inc(
                    (s_xeA, s_xeB)[half], 16)

            def store(turn, half):
                sp.wait_ge(s_ye, STEP * turn + HALF * (half + 1))
                sp.dma_start(tiles_of(yg, turn, half), ye[:, half * HALF:(half + 1) * HALF, :]).then_inc(
                    (s_stA, s_stB)[half], 16)

            def store_out(k):
                first, end = OUTS[k]
                sp.wait_ge(s_out, end)
                sp.dma_start(out_dram[:, first:end, :], x[:, first:end, :]).then_inc(s_stored, 16)

            stored = 0
            load(0, 0)
            load(0, 1)
            for turn in range(TURNS):
                if turn < TURNS - 1:
                    load(turn + 1, 0)
                if turn:
                    store(turn - 1, 1)
                if turn < TURNS - 1:
                    load(turn + 1, 1)
                store(turn, 0)
                if turn > NTURNS[0] and stored < BT[0] // ZT:
                    store_out(stored)
                    stored += 1
            store(TURNS - 1, 1)
            while stored < len(OUTS):
                store_out(stored)
                stored += 1
            sp.wait_ge(s_stored, 16 * len(OUTS))

        @block.gpsimd
        def _(pool):
            nc.gpsimd.memset(zero[:], 0.0).then_inc(s_zero, 1)
            nc.gpsimd.memset(half[:], -0.5).then_inc(s_halves, 1)
            pool.wait_ge(s_we, 16 * N_EXP)
            nc.gpsimd.tensor_copy(w13h[:], w13[:]).then_inc(s_w13, 1)
            pool.wait_ge(s_w13, 1)
            nc.gpsimd.tensor_tensor(w13l[:], w13[:], w13h[:].bitcast(F32), ALU.subtract).then_inc(s_w13, 1)

            def scatter(r, t, i):
                k = BATCHES[r][0] * TG + t
                pool.indirect_dma_start(
                    out=xg[r], out_offset=bass.IndirectOffsetOnAxis(ap=slots[:, i, k:k + 1], axis=0),
                    in_=xn2[:, k, :], in_offset=None).then_inc(s_scat[r], 16)

            pool.wait_ge(s_xgz, 16 * TURNS)
            for r in range(NB):
                if r == 1:
                    pool.wait_ge(s_halves, 1)
                    pool.wait_ge(s_var3e, 1)
                    nc.gpsimd.tensor_tensor(r3[:], var3e[:], half[:], ALU.pow).then_inc(s_r3, 1)
                pool.wait_ge(s_slots, 2 * r + 1)
                pool.wait_ge(s_xn2, BATCHES[r][1] * TG - (TS if r == NB - 1 else 0))
                if r == NB - 1:
                    pool.wait_ge(s_xn2v, TS)
                for t in range(BT[r]):
                    scatter(r, t, 0)
                pool.wait_ge(s_slots, 2 * r + 2)
                for t in range(BT[r]):
                    scatter(r, t, 1)

            def gather(k, r):
                at_least(pool, s_z, k - RING + 1)
                at_least(pool, s_gat[k % ZT], 32 * (k // ZT))
                for i, y_ in enumerate((ya, yb)):
                    pool.indirect_dma_start(
                        out=y_[:, k % RING, :], out_offset=None, in_=yg[r],
                        in_offset=bass.IndirectOffsetOnAxis(ap=slots[:, i, k:k + 1], axis=0),
                    ).then_inc(s_gat[k % ZT], 16)

            for r in range(NB):
                pool.wait_ge(s_stA, 16 * (FIRST[r] + BTURNS[r]))
                pool.wait_ge(s_stB, 16 * (FIRST[r] + BTURNS[r]))
                for k in range(BATCHES[r][0] * TG, BATCHES[r][1] * TG):
                    gather(k, r)
                if r == 0:
                    pool.wait_ge(s_var, 1)
                    nc.gpsimd.tensor_tensor(rz[:, 0:BT[0]], var[:, 0:BT[0]], half[:], ALU.pow).then_inc(s_rz, 1)

        @block.scalar
        def _(act):
            act.dma_start(front[:], front_in).then_inc(s_front, 16)
            act.dma_start(bias[:], bias_in).then_inc(s_bias, 16)
            act.dma_start(back[:], back_in).then_inc(s_back, 16)
            act.wait_ge(s_const, 1)

            def deviations1(part, n):
                act.wait_ge(s_var1, n)
                nc.scalar.activation(sd1[:, part], var1[:, part], ACT.Sqrt, bias=eps[:], scale=1.0 / D).then_inc(s_sd1, 1)

            def norm1(f, first, end):
                act.wait_ge(s_nm1, (1, 2, 2, 3)[f])
                for t in range(first, end):
                    n = f * TG + t
                    nc.scalar.activation(xn[:, t, :], x[:, n, :], ACT.Identity, bias=nm1[:, n:n + 1],
                                         scale=r1[:, n:n + 1]).then_inc(s_xn, 1)

            def deviations2(m):
                act.wait_ge(s_var2, m + 1)
                nc.scalar.activation(sd2[:], var2[:], ACT.Sqrt, bias=eps[:], scale=1.0 / D).then_inc(s_sd2, 1)

            def norm3(b, first, end):
                act.wait_ge(s_nm3, b + 1)
                for t in range(first, end):
                    n = b * TG + t
                    nc.scalar.activation(xn2[:, n, :], x[:, n, :], ACT.Identity, bias=nm3[:, t:t + 1],
                                         scale=r3[:, t:t + 1]).then_inc(s_xn2, 1)

            def step(f, m, b):
                if f is not None:
                    act.wait_ge(s_dft, f + 1)
                    nc.scalar.activation(xft[:], dft_, ACT.Copy).then_inc(s_xft, 1)
                if f == 1:
                    deviations1(slice(3 * TG, NT), 3)
                if b is not None:
                    if b < NG - 1:
                        norm3(b, TS, TG)
                if m is not None and f is not None:
                    deviations2(m)
                if b is not None:
                    for q in range(SEQS):
                        act.wait_ge(s_xn2p, SEQS * b + q + 1)
                        nc.scalar.activation(xn2t[:, q, :], (pb[6 + q] if b == NG - 1 else turned3[q]), ACT.Copy).then_inc(s_xn2t, 1)
                if m is not None and f is None:
                    deviations2(m)
                if f is not None and 0 < f < NG - 1:
                    norm1(f + 1, 0, TS)
                if f is not None:
                    act.wait_ge(s_nmx, f + 1)
                    nc.scalar.activation(ex[:], small[0:NH, 0:M], ACT.Exp, bias=nmx[:], accum_out=exs[:]).then_inc(s_ex, 1)
                    nc.scalar.activation(ex0[:], nmx[:], ACT.Exp).then_inc(s_ex, 1)
                if f is not None and f + 1 < NG:
                    norm1(f + 1, TS if f else 0, TG)
                if m is not None and f is None:
                    high(0, 0)
                    high(1, 1)
                    act.wait_ge(s_gap, NG - 1)
                    nc.scalar.activation(e2[:, 0:NT - TG], gap[:, 0:NT - TG], ACT.Exp, scale=-1.0).then_inc(s_e2, 1)
                    silu(0, 0)
                if m is not None and f is not None:
                    act.wait_ge(s_var3, m + 1)
                    nc.scalar.activation(sd3[:], var3[:], ACT.Sqrt, bias=eps[:], scale=1.0 / D).then_inc(s_sd3, 1)
                if f is not None:
                    act.wait_ge(s_oftp, f + 1)
                    nc.scalar.activation(oft[:], of_t[:, 0:SEQS * P], ACT.Copy).then_inc(s_oft, 1)
                if m is not None:
                    norm3(m, 0, TS)
                if f is not None:
                    act.wait_ge(s_zp, f + 1)
                    nc.scalar.activation(zs[:], z_, ACT.Copy).then_inc(s_zs, 1)

            def high(j, k):
                act.wait_ge(s_xt, j + 1)
                nc.scalar.activation(xh[:, k % 2, :], pb[k % 2][:, 0:P], ACT.Copy).then_inc(s_xh, 1)

            def silu(j, k):
                act.wait_ge(s_gu, j + 1)
                nc.scalar.activation(gate[:, k % 2, :], pb[2 + k % 2][:, 0:F], ACT.Silu).then_inc(s_silu, 1)

            deviations1(slice(0, TG), 1)
            norm1(0, 0, TG)
            deviations1(slice(TG, 3 * TG), 2)
            step(0, None, None)
            step(1, 0, None)
            step(2, 1, 0)
            step(3, 2, 1)
            step(None, NG - 1, NG - 2)
            step(None, None, NG - 1)

            def hidden_out(j, k):
                act.wait_ge(s_ht, j + 1)
                nc.scalar.activation(hidt[:, k % 2, :], pb[4 + k % 2][:, 0:F], ACT.Copy).then_inc(s_hc, 1)

            def tile_out(j, k, turn):
                act.wait_ge(s_dn, j + 1)
                if k == 0:
                    at_least(act, s_stA, 16 * turn)
                if k == HALF:
                    at_least(act, s_stB, 16 * turn)
                nc.scalar.activation(ye[:, k, :], pb[6 + k % 2][:, 0:D], ACT.Copy).then_inc(s_ye, 1)

            def tile_step(j, k, turn, last=False):
                if not (last and k + 1 >= STEP):
                    hidden_out(j + 1, k + 1)
                if not (last and k + AHEAD + 1 >= STEP):
                    high(j + AHEAD + 1, k + AHEAD + 1)
                if not (last and k + AHEAD >= STEP):
                    silu(j + AHEAD, k + AHEAD)
                tile_out(j, k, turn)

            high(2, 2)
            silu(1, 1)
            hidden_out(0, 0)
            high(3, 3)
            silu(2, 2)
            for k in range(STEP):
                tile_step(k, k, 0)
            with act.Fori(1, TURNS - 1) as turn:
                for k in range(STEP):
                    tile_step(turn * STEP + k, k, turn)
            for k in range(STEP):
                tile_step((TURNS - 1) * STEP + k, k, TURNS - 1, last=True)
            act.wait_ge(s_gap, NG)
            nc.scalar.activation(e2[:, NT - TG:], gap[:, NT - TG:], ACT.Exp, scale=-1.0).then_inc(s_e2, 1)

            for i, (first, end) in enumerate(PARTS):
                act.wait_ge(s_sumz, i + 2)
                nc.scalar.activation(sdz[:, first:end], varz[:, first:end], ACT.Sqrt, bias=eps[:],
                                     scale=1.0 / D).then_inc(s_sdz, 1)
                act.wait_ge(s_cz, 2 * (i + 2))
                for k in range(first, end):
                    nc.scalar.activation(zn[:, k, :], za[:, k, :], ACT.Identity, bias=shift[:, k:k + 1],
                                         scale=rz[:, k:k + 1]).then_inc(s_zn, 1)

        @block.vector
        def _(dve):
            V = nc.vector
            V.memset(eps[:], EPS).then_inc(s_const, 1)
            V.memset(ones[:], 1.0).then_inc(s_const, 1)

            def wide(v, n):
                return v.unsqueeze(2).broadcast_to([v.shape[0], v.shape[1], n])

            def every(v, n):
                return v.unsqueeze(1).broadcast_to([v.shape[0], n, v.shape[1]])

            def row(buf, k):
                return buf[:, bass.ds(k, 1), :].rearrange("p a d -> p (a d)")

            def hold(sem_, n):
                dve.wait_ge(sem_, n)
                dve.sem_inc(s_held, 1)

            def moments(st, mean, dif, m2, sq, var_, s_half, s_sq, s_var_, n):
                V.tensor_tensor(mean, st[:, :, 1], st[:, :, 4], ALU.add).then_inc(s_half, 1)
                V.tensor_tensor(dif, st[:, :, 1], st[:, :, 4], ALU.subtract).then_inc(s_half, 1)
                V.tensor_tensor(m2, st[:, :, 2], st[:, :, 5], ALU.add).then_inc(s_half, 1)
                dve.wait_ge(s_half, 3 * n)
                V.scalar_tensor_tensor(sq, dif, D / 4.0, dif, ALU.mult, ALU.mult).then_inc(s_sq, 1)
                dve.wait_ge(s_sq, n)
                V.tensor_tensor(var_, sq, m2, ALU.add).then_inc(s_var_, 1)

            def centre1(first, end, n):
                for g in range(first, end):
                    hold(s_x, 16 * (g + 1))
                    for t in range(g * TG, (g + 1) * TG):
                        V.bn_stats(st1[:, t, :], x[:, t, :]).then_inc(s_st1, 1)
                part = slice(first * TG, end * TG)
                dve.wait_ge(s_st1, end * TG)
                moments(st1[:, part, :], mean1[:, part], dif1[:, part], m2_1[:, part], sq1[:, part], var1[:, part],
                        s_half1, s_sq1, s_var1, n)

            def scales1(first, end, n):
                part = slice(first * TG, end * TG)
                dve.wait_ge(s_sd1, n)
                V.reciprocal(r1[:, part], sd1[:, part]).then_inc(s_r1, 1)
                dve.wait_ge(s_r1, n)
                V.scalar_tensor_tensor(nm1[:, part], mean1[:, part], -0.5, r1[:, part], ALU.mult,
                                       ALU.mult).then_inc(s_nm1, 1)
                dve.wait_ge(s_nm1, n)

            def step(f, m, b):
                if m is not None:
                    for t in range(TG):
                        if t % TS == 0:
                            hold(s_y, SEQS * m + t // TS + 1)
                        V.bn_stats(st2[:, t, :], y[:, t // TS, t % TS * P:(t % TS + 1) * P]).then_inc(s_st2, 1)
                    dve.wait_ge(s_st2, TG * (m + 1))
                    moments(st2, mean2[:], dif2[:], m2_2[:], sq2[:], var2[:], s_half2, s_sq2, s_var2, m + 1)
                if f is not None:
                    filtered(f)
                if f == 0:
                    scales1(1, 3, 2)
                if m is not None:
                    dve.wait_ge(s_sd2, m + 1)
                    V.reciprocal(r2[:], sd2[:]).then_inc(s_r2, 1)
                    dve.wait_ge(s_r2, m + 1)
                    V.scalar_tensor_tensor(shift2[:, m * TG:(m + 1) * TG], mean2[:], -0.5, r2[:],
                                           ALU.mult, ALU.mult)
                if f is None:
                    for i in range(LEAD):
                        residual_piece(m, i)
                    top2(b)
                    for i in range(LEAD + TOP, 2 * TG):
                        residual_piece(m, i)
                for t in range(TG + 1) if f is not None else ():
                    if m is not None:
                        residual(m, t)
                    if f is not None and t == 1:
                        largest(f)
                    if f is not None and t == 2:
                        negated(f)
                    if f == 0 and t == 3:
                        centre1(3, NG, 3)
                    if f is not None and t == 4:
                        total(f)
                    if f is not None and t == 5:
                        inverted(f)
                    if f is not None and t == 6:
                        weighted(f)
                if f == 1:
                    scales1(3, NG, 3)
                if m is not None:
                    dve.wait_ge(s_st3, TG * (m + 1))
                    moments(st3, mean3[:], dif3[:], m2_3[:], sq3[:], var3[:], s_half3, s_sq3, s_var3, m + 1)
                if f is not None:
                    spread(f)
                if m is not None and f is None:
                    dve.wait_ge(s_var3, NG)
                    V.tensor_scalar(var3e[:], var3[:], 1.0 / D, EPS, ALU.mult, ALU.add).then_inc(s_var3e, 1)
                if m is not None and f is not None:
                    inverted3(m)
                    shifts3(m)
                if b is not None and f is not None:
                    top2(b)
                for r in range(NB):
                    if b is not None and b + 1 == BATCHES[r][1]:
                        route(r)

            def x1_of(m, t):
                V.scalar_tensor_tensor(row(x, m * TG + t), y[:, t // TS, t % TS * P:(t % TS + 1) * P],
                                       r2[:, t:t + 1], row(x, m * TG + t), ALU.mult, ALU.add).then_inc(s_x1, 1)

            def x1_moments(m, t):
                hold(s_x1, m * TG + t + 1)
                V.bn_stats(st3[:, t, :], row(x, m * TG + t)).then_inc(s_st3, 1)

            def residual(m, t):
                if t < TG:
                    x1_of(m, t)
                if t > 0:
                    x1_moments(m, t - 1)

            def residual_piece(m, i):
                t = (i + 1) // 2
                if i == 0 or i % 2 == 1 and t < TG:
                    x1_of(m, t)
                else:
                    x1_moments(m, (i - 1) // 2)

            def last_norm3(i):
                if i < 2:
                    low(i, i)
                if i == NORMED:
                    shifts3(NG - 1)
                    dve.wait_ge(s_nm3, NG)
                if i == RT - 1:
                    for t in range(TS, TG):
                        n = (NG - 1) * TG + t
                        V.tensor_scalar(xn2[:, n, :], x[:, n, :], r3[:, t:t + 1], nm3[:, t:t + 1], ALU.mult,
                                        ALU.add).then_inc(s_xn2v, 1)
                    piece(0)

            def inverted3(m):
                dve.wait_ge(s_sd3, m + 1)
                V.reciprocal(r3[:], sd3[:]).then_inc(s_r3, 1)

            def shifts3(m):
                dve.wait_ge(s_r3, m + 1)
                V.scalar_tensor_tensor(nm3[:], mean3[:], -0.5, r3[:], ALU.mult, ALU.mult).then_inc(s_nm3, 1)

            def filtered(f):
                dve.wait_ge(s_qkvp, SEQS * (f + 1))
                V.tensor_tensor(qw[:], qkv[:, :, 0:D], every(fqk[:], SEQS), ALU.mult).then_inc(s_qw, 1)
                V.tensor_tensor(vw[:], qkv[:, :, 2 * D:3 * D], every(fv, SEQS), ALU.mult).then_inc(s_vw, 1)
                dve.wait_ge(s_qw, f + 1)
                V.tensor_tensor(prod[:], qw[:], qkv[:, :, D:2 * D], ALU.mult).then_inc(s_prod, 1)
                dve.wait_ge(s_prod, f + 1)
                V.tensor_reduce(red[:], prod[:].rearrange("p s (h e) -> p (s h) e", e=HD), AX.X,
                                ALU.add).then_inc(s_red, 1)

            def largest(f):
                dve.wait_ge(s_sc, f + 1)
                V.tensor_reduce(mx[:], small[0:NH, 0:M], AX.X, ALU.max).then_inc(s_mx, 1)

            def negated(f):
                dve.wait_ge(s_mx, f + 1)
                V.tensor_scalar(nmx[:], mx[:], 0.0, -1.0, ALU.max, ALU.mult).then_inc(s_nmx, 1)

            def total(f):
                dve.wait_ge(s_ex, 2 * (f + 1))
                V.scalar_tensor_tensor(tot[:], ex0[:], CUT, exs[:], ALU.mult, ALU.add).then_inc(s_tot, 1)

            def inverted(f):
                dve.wait_ge(s_tot, f + 1)
                V.reciprocal(rtot[:], tot[:]).then_inc(s_rtot, 1)

            def weighted(f):
                dve.wait_ge(s_rtot, f + 1)
                V.tensor_scalar(attn[:], every(ex[:], 2), rtot[:, 0:1], None, ALU.mult).then_inc(s_attn, 1)

            def spread(f):
                dve.wait_ge(s_at, f + 1)
                dve.wait_ge(s_vw, f + 1)
                V.tensor_tensor(of[:].rearrange("p s (h e) -> p (s h) e", e=HD),
                                vw[:].rearrange("p s (h e) -> p (s h) e", e=HD),
                                wide(small[:, M:M + NH], HD), ALU.mult).then_inc(s_of, 1)

            def low(j, k):
                dve.wait_ge(s_xh, j + 1)
                V.tensor_tensor(xl[:, k % 2, :], pb[k % 2][:, 0:P], xh[:, k % 2, :].bitcast(F32),
                                ALU.subtract).then_inc(s_xl, 1)

            def hidden(j, k):
                dve.wait_ge(s_silu, j + 1)
                V.tensor_tensor(hid[:, k % 2, :], pb[2 + k % 2][:, F:2 * F], gate[:, k % 2, :],
                                ALU.mult).then_inc(s_h, 1)

            def piece(i):
                if i % 2 == 0:
                    hidden(i // 2, i // 2)
                else:
                    low(i // 2 + 2, i // 2 + 2)


            def place(b):
                return (b - max(first for first, _ in BATCHES if first <= b)) * TG

            def top2(b):
                dve.wait_ge(s_lg, b + 1)
                logits = (last_logits[:] if b == NG - 1 else route_[:, 0:TG * E]).rearrange("p (t e) -> p t e", e=E)
                n = TOP * b
                at = place(b)
                oh1_, oh2_ = oh1[:, at:at + TG, :], oh2[:, at:at + TG, :]

                def then(ins):
                    nonlocal n
                    ins.then_inc(s_top, 1)
                    if b == NG - 2:
                        residual_piece(NG - 1, LEAD + n % TOP)
                    if b == NG - 1 and n % TOP % 2 == 1:
                        piece(EARLY + n % TOP // 2)
                    n = n + 1
                    dve.wait_ge(s_top, n)

                then(V.tensor_reduce(m1[:], logits, AX.X, ALU.max))
                then(V.tensor_tensor(eq[:], logits, wide(m1[:], E), ALU.is_equal))
                then(V.tensor_tensor(eqd[:], eq[:], every(e_down, TG), ALU.mult))
                then(V.tensor_reduce(i1[:], eqd[:], AX.X, ALU.max))
                then(V.tensor_tensor(oh1_, every(e_down, TG), wide(i1[:], E), ALU.is_equal))
                then(V.scalar_tensor_tensor(rest[:], oh1_, -BIG, logits, ALU.mult, ALU.add))
                then(V.tensor_reduce(m2[:], rest[:], AX.X, ALU.max))
                then(V.tensor_tensor(eq[:], rest[:], wide(m2[:], E), ALU.is_equal))
                then(V.tensor_tensor(eqd[:], eq[:], every(e_down, TG), ALU.mult))
                then(V.tensor_reduce(i2[:], eqd[:], AX.X, ALU.max))
                then(V.tensor_tensor(oh2_, every(e_down, TG), wide(i2[:], E), ALU.is_equal))
                V.tensor_tensor(gap[:, bass.ds(b * TG, TG)], m1[:], m2[:], ALU.subtract).then_inc(s_gap, 1)
                for r in range(NB):
                    if b + 1 == BATCHES[r][1]:
                        V.tensor_tensor(cnt[:, 0:E * BT[r]].rearrange("p (e t) -> p t e", t=BT[r]),
                                        oh1[:, 0:BT[r], :], oh2[:, 0:BT[r], :], ALU.add).then_inc(s_cnt, 1)

            def route(r):
                n, nt = RT * r, BT[r]
                first, tiles_of_batch = BATCHES[r][0] * TG, BTURNS[r] * STEP

                def then(ins):
                    nonlocal n
                    ins.then_inc(s_rt, 1)
                    if r == 1:
                        last_norm3(n % RT)
                    if r == NB - 1 and ROUTED + n % RT < 2 * (STEP + AHEAD) - 1:
                        piece(ROUTED + n % RT)
                    n = n + 1
                    dve.wait_ge(s_rt, n)

                def flat(v):
                    return v[:, 0:E * nt]

                def by_expert(v):
                    return flat(v).rearrange("p (e t) -> p e t", t=nt)

                def by_tile(v):
                    return flat(v).rearrange("p (e t) -> p t e", t=nt)

                if r == NB - 1:
                    prefix, totals = last_sums[:, 0, :], last_sums[:, 1, :]
                else:
                    prefix, totals = route_[:, 64:64 + E * nt], route_[:, 64 + E * MOST:64 + E * MOST + E * nt]
                    dve.wait_ge(s_pfx, r + 1)
                then(V.tensor_tensor_scan(flat(inc), t_keep[nt], totals, 0.0, ALU.mult, ALU.add))
                then(V.tensor_scalar(up[:], by_expert(inc)[:, :, nt - 1], float(P - 1), None, ALU.add))
                then(V.tensor_scalar(tiles[:], up[:], 7, None, ALU.arith_shift_right))
                then(V.tensor_tensor_scan(cum[:], ones[:, 0:E], tiles[:], 0.0, ALU.mult, ALU.add))
                then(V.tensor_tensor(base[:], cum[:], tiles[:], ALU.subtract))
                then(V.tensor_tensor(flat(pos), flat(inc), totals, ALU.subtract))
                then(V.tensor_tensor(flat(pos2), flat(pos), prefix, ALU.add))
                then(V.scalar_tensor_tensor(by_expert(slot), wide(base[:], nt), float(P), by_expert(pos2),
                                            ALU.mult, ALU.add))
                then(V.tensor_tensor(pick1[:, 0:nt, :], oh1[:, 0:nt, :], by_tile(slot), ALU.mult))
                V.tensor_reduce(slots[:, 0, first:first + nt], pick1[:, 0:nt, :], AX.X, ALU.add).then_inc(s_slots, 1)
                then(V.tensor_tensor(pick2[:, 0:nt, :], oh2[:, 0:nt, :], by_tile(slot), ALU.mult))
                V.tensor_reduce(slots[:, 1, first:first + nt], pick2[:, 0:nt, :], AX.X, ALU.add).then_inc(s_slots, 1)
                ends = before[:, 0:tiles_of_batch * 7].rearrange("p (j e) -> p j e", e=7)
                then(V.tensor_tensor(ends, every(cum[0:1, 0:7], tiles_of_batch),
                                     j_row[0:1, 0:tiles_of_batch * 7].rearrange("p (j e) -> p j e", e=7), ALU.is_le))
                V.tensor_reduce(expert[:, 0:tiles_of_batch], ends, AX.X, ALU.add).then_inc(s_cols, 1)
                dve.wait_ge(s_cols, 2 * r + 1)
                V.tensor_scalar(columns[:, FIRST[r] * STEP:FIRST[r] * STEP + tiles_of_batch],
                                expert[:, 0:tiles_of_batch], float(2 * F), None, ALU.mult).then_inc(s_cols, 1)

            centre1(0, 1, 1)
            scales1(0, 1, 1)
            dve.wait_ge(s_front, 16)
            V.tensor_tensor(fold[:, :], ident[:, 0:M], ident[:, M:2 * M], ALU.add).then_inc(s_const, 1)
            V.tensor_tensor(fqk[:], fq, fk, ALU.mult).then_inc(s_fqk, 1)
            dve.wait_ge(s_bias, 16)
            V.tensor_scalar(bqkv[:], bias[:, BIAS["bqkv"]], float(S), None, ALU.mult).then_inc(s_const, 1)
            dve.wait_ge(s_fqk, 1)
            centre1(1, 3, 2)
            step(0, None, None)
            dve.wait_ge(s_back, 16)
            V.tensor_copy(tri[:], tri_f).then_inc(s_const, 1)
            step(1, 0, None)
            step(2, 1, 0)
            step(3, 2, 1)
            def first_row(k, which):
                dve.wait_ge(s_gat[which], (k >> 2) * 32 + 32)
                V.tensor_scalar(row(za, k), row(ya, wrap(k)), wt1[:, bass.ds(k, 1)], None, ALU.mult).then_inc(s_za, 1)

            def second_row(k):
                dve.wait_ge(s_za, k + 1)
                V.scalar_tensor_tensor(row(za, k), row(yb, wrap(k)), wt2[:, bass.ds(k, 1)], row(za, k),
                                       ALU.mult, ALU.add).then_inc(s_z, 1)

            def sum_moments(k):
                hold(s_z, k + 1)
                V.bn_stats(row(stz, k), row(za, k)).then_inc(s_stz, 1)

            def wrap(k):
                return k & (RING - 1)

            def variances(n, first, end):
                part = slice(first, end)
                dve.wait_ge(s_stz, end)
                moments(stz[:, part, :], meanz[:, part], difz[:, part], m2_z[:, part], sqz[:, part],
                        varz[:, part], s_halfz, s_sqz, s_sumz, n + 1)

            def inverted_deviations(n, first, end):
                part = slice(first, end)
                dve.wait_ge(s_sdz, n)
                V.reciprocal(rz[:, part], sdz[:, part]).then_inc(s_rz2, 1)
                dve.wait_ge(s_rz2, n)

            def shifts(n, first, end):
                part = slice(first, end)
                V.scalar_tensor_tensor(cz[:, part], meanz[:, part], -0.5, rz[:, part], ALU.mult,
                                       ALU.mult).then_inc(s_cz, 1)
                dve.wait_ge(s_cz, 2 * n + 1)
                V.tensor_tensor(shift[:, part], cz[:, part], shift2[:, part], ALU.add).then_inc(s_cz, 1)

            def added(k):
                dve.wait_ge(s_zn, k + 1)
                V.tensor_tensor(x[:, k, :], zn[:, k, :], x[:, k, :], ALU.add).then_inc(s_out, 1)

            def norm_of(n, finished=()):
                variances(n, *PARTS[n - 1])
                for k in finished:
                    added(k)
                inverted_deviations(n, *PARTS[n - 1])
                shifts(n, *PARTS[n - 1])

            def scaled(k):
                V.scalar_tensor_tensor(row(zn, k), row(za, k), rz[:, bass.ds(k, 1)], row(x, k), ALU.mult,
                                       ALU.add).then_inc(s_zn, 1)

            def shifted(k):
                dve.wait_ge(s_zn, k + 1)
                V.tensor_scalar(row(x, k), row(zn, k), shift[:, bass.ds(k, 1)], None, ALU.add).then_inc(s_out, 1)

            def sums_of(tiles_, finished=()):
                n = len(tiles_)
                for i in range(n + 2):
                    for k in finished[2 * i:2 * i + 2]:
                        added(k)
                    if i < n:
                        first_row(tiles_[i], tiles_[i] % ZT)
                    if 0 <= i - 1 < n:
                        second_row(tiles_[i - 1])
                    if 0 <= i - 2 < n:
                        sum_moments(tiles_[i - 2])

            def turn_of(turn, summed=None, normed=None, last=False):
                for k in range(STEP):
                    if not (last and k + AHEAD + 1 >= STEP):
                        low(turn * STEP + k + AHEAD + 1, k + AHEAD + 1)
                    if summed is not None and k % 2 == 0:
                        first_row(summed + k // 2, k // 2)
                    if summed is not None and k % 2 == 1:
                        second_row(summed + k // 2)
                    if not (last and k + AHEAD >= STEP):
                        hidden(turn * STEP + k + AHEAD, k + AHEAD)
                    if summed is not None and k % 2 == 1:
                        sum_moments(summed + k // 2)
                    if normed is not None and k % 2 == 0:
                        scaled(normed + k // 2)
                    if normed is not None and k % 2 == 1:
                        shifted(normed + k // 2)

            def weights(part, n):
                dve.wait_ge(s_e2, n)
                V.tensor_scalar(e2p[:, part], e2[:, part], 1.0, None, ALU.add).then_inc(s_wt, 1)
                dve.wait_ge(s_wt, 3 * n - 2)
                V.reciprocal(wt1[:, part], e2p[:, part]).then_inc(s_wt, 1)
                dve.wait_ge(s_wt, 3 * n - 1)
                V.tensor_tensor(wt2[:, part], wt1[:, part], e2[:, part], ALU.mult).then_inc(s_wt, 1)
                dve.wait_ge(s_wt, 3 * n)

            step(None, NG - 1, NG - 2)
            weights(slice(0, NT - TG), 1)
            for i in range(1, EARLY):
                piece(i)
            dve.wait_ge(s_lg, NG)
            V.tensor_copy(last_logits[:], pb[6][:, 0:TG * E]).then_inc(s_last, 1)
            dve.wait_ge(s_last, 1)
            top2(NG - 1)
            for i in range(EARLY + TOP // 2, ROUTED):
                piece(i)
                if i == PREFIX:
                    dve.wait_ge(s_pfx, NB)
                    V.tensor_copy(last_sums[:], pb[0][:, P:P + 2 * E * TG].rearrange("p (a n) -> p a n", a=2)
                                  ).then_inc(s_last, 1)
                    dve.wait_ge(s_last, 2)
            route(NB - 1)
            for i in range(ROUTED + RT, 2 * (STEP + AHEAD) - 1):
                piece(i)
            with dve.Fori(1, ZTURNS[0]) as turn:
                turn_of(turn)
            with dve.Fori(ZTURNS[0], ZTURNS[1]) as turn:
                turn_of(turn, summed=(turn - ZTURNS[0]) * ZT)
            variances(0, 0, BT[0])
            dve.wait_ge(s_sumz, 1)
            V.tensor_scalar(var[:, 0:BT[0]], varz[:, 0:BT[0]], 1.0 / D, EPS, ALU.mult, ALU.add).then_inc(s_var, 1)
            with dve.Fori(ZTURNS[1], NTURNS[0]) as turn:
                turn_of(turn)
            dve.wait_ge(s_rz, 1)
            shifts(0, 0, BT[0])
            dve.wait_ge(s_cz, 2)
            with dve.Fori(NTURNS[0], NTURNS[1]) as turn:
                turn_of(turn, normed=(turn - NTURNS[0]) * ZT)
            with dve.Fori(LATE, TURNS - 1) as turn:
                turn_of(turn, summed=(turn - LATE) * ZT + BT[0])
            turn_of(TURNS - 1, summed=(TURNS - 1 - LATE) * ZT + BT[0], last=True)
            weights(slice(NT - TG, NT), 2)
            sums_of(range(BT[0] + (TURNS - LATE) * ZT, BT[0] + BT[1]))
            norm_of(1)
            sums_of(range(*PARTS[1]), range(*PARTS[0]))
            norm_of(2)
            sums_of(range(*PARTS[2]))
            norm_of(3, range(*PARTS[1]))
            for k in range(*PARTS[2]):
                added(k)

        @block.tensor
        def _(pe):
            T = nc.tensor

            def keep_busy(n, bank_):
                for _ in range(n):
                    T.matmul(bank_[:, 512 - P:512], ones[:], ones[:], start=True, stop=True)

            pe.wait_ge(s_const, 2)
            keep_busy(WAIT_START, pb[5])
            pe.wait_ge(s_front, 16)
            pe.wait_ge(s_const, 4)

            def turn3(b, banks=turned3):
                for q in range(SEQS):
                    if b == NG - 1 and q == 1:
                        pe.wait_ge(s_xn2v, TS)
                    else:
                        pe.wait_ge(s_xn2, TG * b + TS * (q + 1))
                    for t in range(TS):
                        ins = T.transpose(banks[q][:, t * P:(t + 1) * P], xn2[:, b * TG + q * TS + t, :], ident)
                    ins.then_inc(s_xn2p, 1)

            def logits(b, bank_):
                for q in range(SEQS):
                    pe.wait_ge(s_xn2t, SEQS * b + q + 1)
                    for t in range(TS):
                        n = q * TS + t
                        ins = T.matmul(bank_[:, n * E:(n + 1) * E], xn2t[:, q, t * P:(t + 1) * P], rw,
                                       start=True, stop=True)
                ins.then_inc(s_lg, 1)

            def sums(r, prefix, totals):
                pe.wait_ge(s_cnt, r + 1)
                flat = cnt[:, 0:E * BT[r]]
                T.matmul(prefix, tri[:], flat, start=True, stop=True)
                T.matmul(totals, ones[:], flat, start=True, stop=True).then_inc(s_pfx, 1)

            def transform(f, q):
                pe.wait_ge(s_xn, TG * f + TS * (q + 1))
                for t in range(TS):
                    ins = T.matmul(dft_[:, q * P:(q + 1) * P], xn[:, q * TS + t, :], ftab[:, t, :],
                                   start=(t == 0), stop=(t == TS - 1))
                if q == SEQS - 1:
                    ins.then_inc(s_dft, 1)

            def step(f, m, b):
                if m is not None:
                    keep_busy(WAIT_Z, pb[4])
                    pe.wait_ge(s_zs, m + 1)
                    for q in range(SEQS):
                        for t in range(TS):
                            ins = T.matmul(y[:, q, t * P:(t + 1) * P], ginv[:, t * P:(t + 1) * P], zs[:, q, :],
                                           start=True, stop=True)
                        ins.then_inc(s_y, 1)
                if f is not None:
                    for q in range(SEQS):
                        T.matmul(qkv[:, q, 0:3 * D], ident[0:1, :], bqkv[:], start=True, stop=False)
                    pe.wait_ge(s_xft, f + 1)
                    for q in range(SEQS):
                        T.matmul(qkv[:, q, 0:3 * D], xft[:, q, :], wqkv, start=False, stop=True).then_inc(s_qkvp, 1)
                if b is not None:
                    turn3(b)
                if f is not None:
                    keep_busy(WAIT_RED, pb[1])
                    pe.wait_ge(s_red, f + 1)
                    T.matmul(small[0:NH, 0:M], red[:], fold[:], start=True, stop=True).then_inc(s_sc, 1)
                if b is not None:
                    at_least(pe, s_slots, 2 * sum(end <= b for _, end in BATCHES))
                    at_least(pe, s_top, TOP * b)
                    logits(b, route_)
                if f is not None and 0 < f < NG - 1:
                    transform(f + 1, 0)
                if f is not None:
                    keep_busy(WAIT_ATTENTION, pb[0])
                    pe.wait_ge(s_attn, f + 1)
                    T.matmul(small[:, M:M + NH], attn[:].rearrange("h a m -> h (a m)"), ident[0:NH, 0:NH],
                             start=True, stop=True).then_inc(s_at, 1)
                    keep_busy(WAIT_OF, pb[0])
                    pe.wait_ge(s_of, f + 1)
                    for q in range(SEQS):
                        ins = T.transpose(of_t[:, q * P:(q + 1) * P], of[:, q, :], ident)
                    ins.then_inc(s_oftp, 1)
                if f == 0:
                    transform(1, 0)
                if f is not None and f + 1 < NG:
                    transform(f + 1, 1)
                if f is not None:
                    for q in range(SEQS):
                        T.matmul(z_[:, q * P:(q + 1) * P], ident[0:1, :], bout, start=True, stop=False)
                        if q == 0:
                            pe.wait_ge(s_oft, f + 1)
                        ins = T.matmul(z_[:, q * P:(q + 1) * P], oft[:, q, :], wout, start=False, stop=True)
                    ins.then_inc(s_zp, 1)
                if f is None:
                    keep_busy(WAIT_COUNTS, pb[4])
                    turned(0, 0, 0)
                    turned(1, 1, 0)
                    keep_busy(WAIT_LOW, pb[4])
                for r in range(NB):
                    if b is not None and b + 1 == BATCHES[r][1]:
                        sums(r, route_[:, 64:64 + E * BT[r]], route_[:, 64 + E * MOST:64 + E * (MOST + BT[r])])

            def turned(j, k, turn):
                if k % STEP == 0:
                    pe.wait_ge(s_xeA, 16 * (turn + 1))
                if k % STEP == HALF:
                    pe.wait_ge(s_xeB, 16 * (turn + 1))
                T.transpose(pb[k % 2][:, 0:P], xe[:, k % STEP, :], ident).then_inc(s_xt, 1)

            cols = [pe.alloc_register(f"columns_{k}") for k in range(STEP + AHEAD)]

            def experts_of(turn, n):
                pe.load(cols[0:n], columns[0:1, bass.ds(turn * STEP, n)])
                return [pe.snap(r, min_val=0, max_val=(E - 1) * 2 * F) for r in cols[0:n]]

            def gate_up(j, k, col):
                pe.wait_ge(s_xl, j + 1)
                out_, c = pb[2 + k % 2][:], k % 2
                hi, lo = w13h[:, bass.ds(col, 2 * F)], w13l[:, bass.ds(col, 2 * F)]
                T.matmul(out_, xh[:, c, :], hi, start=True, stop=False)
                T.matmul(out_, xh[:, c, :], lo, start=False, stop=False)
                T.matmul(out_, xl[:, c, :], hi, start=False, stop=True).then_inc(s_gu, 1)

            transform(0, 0)
            transform(0, 1)
            pe.wait_ge(s_back, 16)
            step(0, None, None)
            pe.wait_ge(s_const, 5)
            step(1, 0, None)
            step(2, 1, 0)
            step(3, 2, 1)
            step(None, NG - 1, NG - 2)
            def hidden_turned(j, k):
                pe.wait_ge(s_h, j + 1)
                for c in range(FC):
                    ins = T.transpose(pb[4 + k % 2][:, c * P:(c + 1) * P], hid[:, k % 2, c * P:(c + 1) * P], ident)
                ins.then_inc(s_ht, 1)

            def down(j, k, col):
                pe.wait_ge(s_hc, j + 1)
                for c in range(FC):
                    ins = T.matmul(pb[6 + k % 2][:, 0:D], hidt[:, k % 2, c * P:(c + 1) * P],
                                   w2[:, bass.ds(col + c * D, D)], start=(c == 0), stop=(c == FC - 1))
                ins.then_inc(s_dn, 1)

            def transposes(j, k, turn, last=False):
                if not (last and k + 1 >= STEP):
                    hidden_turned(j + 1, k + 1)
                if not (last and k + AHEAD + 1 >= STEP):
                    turned(j + AHEAD + 1, k + AHEAD + 1, turn + (k + AHEAD + 1) // STEP)

            def products(j, k, exp, last=False):
                if not (last and k + AHEAD >= STEP):
                    gate_up(j + AHEAD, k + AHEAD, exp[k + AHEAD])
                down(j, k, exp[k])

            pe.wait_ge(s_w13, 2)
            pe.wait_ge(s_we, 16 * N_EXP)
            pe.wait_ge(s_cols, 2)
            exp = experts_of(0, STEP + AHEAD)
            gate_up(0, 0, exp[0])
            gate_up(1, 1, exp[1])
            keep_busy(WAIT_LAST, pb[4])
            turn3(NG - 1, (pb[6], pb[7]))
            turned(2, 2, 0)
            hidden_turned(0, 0)
            logits(NG - 1, pb[6])
            turned(3, 3, 0)
            gate_up(2, 2, exp[2])
            pe.wait_ge(s_last, 1)
            for k in range(STEP):
                if k == 2:
                    pe.wait_ge(s_xl, 5)
                    sums(NB - 1, pb[0][:, P:P + E * TG], pb[0][:, P + E * TG:P + 2 * E * TG])
                transposes(k, k, 0)
                products(k, k, exp)
            with pe.Fori(1, TURNS - 1) as turn:
                for k in range(STEP):
                    transposes(turn * STEP + k, k, turn)
                    if k == HALF:
                        pe.wait_ge(s_cols, 2 * NB)
                    if k == 0:
                        exp = experts_of(turn, STEP + AHEAD)
                    products(turn * STEP + k, k, exp)
            for k in range(STEP):
                j = (TURNS - 1) * STEP + k
                transposes(j, k, TURNS - 1, last=True)
                if k == 0:
                    exp = experts_of(TURNS - 1, STEP)
                products(j, k, exp, last=True)


def kernel(L0_attn_query, L0_attn_w_qkv, L0_attn_b_qkv, L0_attn_w_out, L0_attn_b_out, L0_attn_freq_q,
           L0_attn_freq_k, L0_attn_freq_v, L0_ffn_router_w, L0_ffn_w1, L0_ffn_w3, L0_ffn_w2):
    import concourse.bacc as bacc
    from concourse.bass_utils import run_bass_kernel_spmd

    f32 = np.float32

    def both_halves(w):
        w = np.transpose(np.asarray(w), (1, 0, 2)).reshape(M, D)
        return np.concatenate([w, w], axis=0)

    angle = 2 * np.pi * (np.outer(np.arange(S), np.arange(M)) % S) / S
    ftab = np.concatenate([np.cos(angle), np.sin(angle)], axis=1).astype(f32)
    w_qkv, w_out = np.asarray(L0_attn_w_qkv), np.asarray(L0_attn_w_out)
    front = {"ftab": ftab.reshape(TS, P, P).transpose(1, 0, 2).reshape(P, TS * P), "wqkv": w_qkv.T,
             "ident": np.eye(P, dtype=f32), "fq": both_halves(L0_attn_freq_q), "fk": both_halves(L0_attn_freq_k),
             "fv": both_halves(L0_attn_freq_v)}
    tile = np.repeat(np.arange(ET), E - 1)
    back = {"ginv": ftab.T, "wout": w_out.T, "rw": np.asarray(L0_ffn_router_w),
            "tri": np.triu(np.ones((P, P), f32), 1), "down": np.tile(8 - np.arange(E, dtype=f32), (P, 1)),
            "keep_small": np.tile((np.arange(TG) > 0).astype(f32), (P, E)),
            "keep": np.tile((np.arange(MOST) > 0).astype(f32), (P, E)), "tile": np.tile(tile.astype(f32), (P, 1))}
    bias = np.concatenate([np.asarray(L0_attn_b_qkv), np.asarray(L0_attn_b_out)])[None]
    w1, w3, w2 = (np.asarray(w) for w in (L0_ffn_w1, L0_ffn_w3, L0_ffn_w2))
    arrays = {
        "query": np.asarray(L0_attn_query).reshape(B * S, D),
        "front": np.concatenate([front[name] for name in FRONT], axis=1),
        "back": np.concatenate([back[name] for name in BACK], axis=1),
        "bias": bias,
        "w13": np.concatenate([w1, w3], axis=2).transpose(1, 0, 2).reshape(D, E * 2 * F),
        "w2": w2.reshape(E, FC, P, D).transpose(2, 0, 1, 3).reshape(P, E * FC * D),
    }
    nc = bacc.Bacc("TRN2", target_bir_lowering=False, num_devices=1)
    ins, args = {}, []
    for name, a in arrays.items():
        ins[f"in_{name}"] = np.ascontiguousarray(a)
        args.append(nc.dram_tensor(f"in_{name}", a.shape, mybir.dt.from_np(a.dtype), kind="ExternalInput").ap())
    out = nc.dram_tensor("out_x", (B * S, D), F32, kind="ExternalOutput").ap()
    build(nc, *args, out)
    r = run_bass_kernel_spmd(nc, [ins], core_ids=[0])
    return r.results[0]["out_x"].reshape(B, S, D)
```
